# Optimizing a Trainium2 kernel written in Bass

```python
import numpy as np
import jax
import jax.numpy as jnp

def _softmax(x, axis=-1):
    return jax.nn.softmax(x, axis=axis)

def _gelu(x):
    return jax.nn.gelu(x, approximate=True)

def _silu(x):
    return jax.nn.silu(x)

def _sigmoid(x):
    return jax.nn.sigmoid(x)

def _layernorm(x, axis=-1, eps=1e-05):
    m = jnp.mean(x, axis=axis, keepdims=True)
    v = jnp.var(x, axis=axis, keepdims=True)
    return (x - m) / jnp.sqrt(v + eps)

def _scatter_add(tgt, idx, src, axis=0):
    return tgt.at[idx].add(src)

def _segment_sum(src, seg, n):
    return jax.ops.segment_sum(src, seg, n)
kernel_name = 'mk_xattn_ffn_d2_seqx_r8_39a107'

def setup_inputs(seed: int=0):
    np.random.seed(seed)
    _w = jnp.asarray

    def _rec_inputs():
        import jax
        import jax.numpy as jnp
        _rk = jax.random.key(seed)
        x = 7.22e-05 + 1 * jax.random.normal(jax.random.fold_in(_rk, 1), (64, 64, 256), jnp.float32)
        _lenS = 64 - jax.random.randint(jax.random.fold_in(_rk, 7), (64,), 0, max(1, 64 // 4) + 1, jnp.int32)
        _lenS2 = 64 - jax.random.randint(jax.random.fold_in(_rk, 8), (64,), 0, max(1, 64 // 4) + 1, jnp.int32)
        _ctx_1024P = jax.random.normal(jax.random.fold_in(_rk, 11), (64, 16, 128), jnp.float32)
        _ctx_1024c = jax.random.dirichlet(jax.random.fold_in(_rk, 511), 0.3 * jnp.ones((16,), jnp.float32), (64, 64))
        _ctx_1024t = jnp.einsum('bsk,bkd->bsd', _ctx_1024c, _ctx_1024P)
        _ctx_1024t = _ctx_1024t * jax.lax.rsqrt(jnp.mean(jnp.square(_ctx_1024t)) + 1e-12) * 0.953939
        ctx_1024 = -1.39393e-06 + 0.999914 * (_ctx_1024t + 0.3 * jax.random.normal(jax.random.fold_in(_rk, 611), (64, 64, 128), jnp.float32))
        fside_BxSx2_0 = jax.random.uniform(jax.random.fold_in(_rk, 12), (64, 64, 2), jnp.float32, 0.0, 0.999707)
        return (x, ctx_1024, fside_BxSx2_0)
    x, ctx_1024, fside_BxSx2_0 = _rec_inputs()

    def _L0_xattn_setup():
        import jax, jax.numpy as jnp
        import numpy as np
        DIM = 256
        CTX_DIM = 128
        N_HEADS = 32
        HEAD_DIM = DIM // N_HEADS
        POS_DIM = 2
        B, N, CTXN = (2, 256, 256)
        ROPE_BASE = 10000.0

        def apply_axial_rope(x, pos):
            b, n, h, d = x.shape
            p = pos.shape[-1]
            dpa = d // p
            half = dpa // 2
            freqs = ROPE_BASE ** (-jnp.arange(half, dtype=x.dtype) / half)
            ang = pos[..., :, None] * freqs
            cos = jnp.cos(ang)[:, :, None, :, :]
            sin = jnp.sin(ang)[:, :, None, :, :]
            xr = x.reshape(b, n, h, p, half, 2)
            x1, x2 = (xr[..., 0], xr[..., 1])
            out = jnp.stack([x1 * cos - x2 * sin, x1 * sin + x2 * cos], axis=-1)
            return out.reshape(b, n, h, d)
        key = jax.random.key(seed)
        ks = jax.random.split(key, 8)
        x = jax.random.normal(ks[0], (B, N, DIM), jnp.float32)
        ctx = jax.random.normal(ks[1], (B, CTXN, CTX_DIM), jnp.float32)
        pos_map = jax.random.uniform(ks[2], (B, N, POS_DIM), jnp.float32)
        ctx_pos_map = jax.random.uniform(ks[3], (B, CTXN, POS_DIM), jnp.float32)
        Wq = jax.random.normal(ks[4], (DIM, DIM), jnp.float32) / np.sqrt(DIM)
        Wkv = jax.random.normal(ks[5], (CTX_DIM, 2 * DIM), jnp.float32) / np.sqrt(CTX_DIM)
        Wout = jax.random.normal(ks[6], (DIM, DIM), jnp.float32) / np.sqrt(DIM)
        bout = jnp.zeros((DIM,), jnp.float32)
        return {'x': x, 'ctx': ctx, 'pos_map': pos_map, 'ctx_pos_map': ctx_pos_map, 'Wq': Wq, 'Wkv': Wkv, 'Wout': Wout, 'bout': bout}
    _L0_xattn_all = _L0_xattn_setup()
    _L0_xattn_in = {k: v for k, v in _L0_xattn_all.items() if k in ('Wq', 'Wkv', 'Wout', 'bout')}
    del _L0_xattn_all

    def _L0_ffn_setup():
        import jax, jax.numpy as jnp
        import numpy as np
        B, L, D = (4, 512, 256)
        DF = 4 * D
        CAPACITY_RATIO = 0.5
        key = jax.random.key(seed)
        ks = jax.random.split(key, 4)
        s = 0.02
        return {'x': jax.random.normal(ks[0], (B, L, D), dtype=jnp.float32), 'w_r': jax.random.normal(ks[1], (D,), dtype=jnp.float32) * s, 'b_r': jnp.zeros((), dtype=jnp.float32), 'w1': jax.random.normal(ks[2], (D, DF), dtype=jnp.float32) * s, 'b1': jnp.zeros((DF,), dtype=jnp.float32), 'w2': jax.random.normal(ks[3], (DF, D), dtype=jnp.float32) * s, 'b2': jnp.zeros((D,), dtype=jnp.float32)}
    _L0_ffn_all = _L0_ffn_setup()
    _L0_ffn_in = {k: v for k, v in _L0_ffn_all.items() if k in ('w_r', 'b_r', 'w1', 'b1', 'w2', 'b2')}
    del _L0_ffn_all

    def _L1_xattn_setup():
        import jax, jax.numpy as jnp
        import numpy as np
        B, S1, S2, DCA = (2, 256, 128, 16)
        QDIM, KDIM, H = (256, 128, 16)
        HD = QDIM // H
        SCALE = HD ** (-0.5)
        EPS = 1e-06
        DCA_WEIGHT = 1.0

        def _ln(t, w, b):
            m = jnp.mean(t, axis=-1, keepdims=True)
            v = jnp.var(t, axis=-1, keepdims=True)
            return (t - m) * jax.lax.rsqrt(v + EPS) * w + b

        def _attn(q, k, v):
            s = jnp.einsum('bhqd,bhkd->bhqk', q, k) * SCALE
            p = jax.nn.softmax(s, axis=-1)
            return jnp.einsum('bhqk,bhkd->bhqd', p, v)
        key = jax.random.key(seed)
        ks = jax.random.split(key, 8)
        w = lambda k, shape: jax.random.normal(k, shape, jnp.float32) * 0.02
        return {'x': jax.random.normal(ks[0], (B, S1, QDIM), jnp.float32), 'y': jax.random.normal(ks[1], (B, S2 + DCA, KDIM), jnp.float32), 'Wq': w(ks[2], (QDIM, QDIM)), 'bq': jnp.zeros((QDIM,), jnp.float32), 'Wk': w(ks[3], (KDIM, QDIM)), 'bk': jnp.zeros((QDIM,), jnp.float32), 'Wv': w(ks[4], (KDIM, QDIM)), 'bv': jnp.zeros((QDIM,), jnp.float32), 'Wkv_dca': w(ks[5], (KDIM, 2 * QDIM)), 'bkv_dca': jnp.zeros((2 * QDIM,), jnp.float32), 'qn_w': jnp.ones((HD,), jnp.float32), 'qn_b': jnp.zeros((HD,), jnp.float32), 'kn_w': jnp.ones((HD,), jnp.float32), 'kn_b': jnp.zeros((HD,), jnp.float32), 'kn_dca_w': jnp.ones((HD,), jnp.float32), 'kn_dca_b': jnp.zeros((HD,), jnp.float32), 'Wo': w(ks[6], (QDIM, QDIM)), 'bo': jnp.zeros((QDIM,), jnp.float32)}
    _L1_xattn_all = _L1_xattn_setup()
    _L1_xattn_in = {k: v for k, v in _L1_xattn_all.items() if k in ('Wq', 'bq', 'Wk', 'bk', 'Wv', 'bv', 'Wkv_dca', 'bkv_dca', 'qn_w', 'qn_b', 'kn_w', 'kn_b', 'kn_dca_w', 'kn_dca_b', 'Wo', 'bo')}
    del _L1_xattn_all

    def _L1_ffn_setup():
        import jax, jax.numpy as jnp
        import numpy as np
        E = 64
        K = 8
        H = 256
        I = 96
        CAP = 64

        def _moe(hidden_states, gate_w, wg, wu, wd):
            B, S, Hd = hidden_states.shape
            x = hidden_states.reshape(-1, Hd)
            T = x.shape[0]
            logits = x @ gate_w.T
            probs = jax.nn.softmax(logits.astype(jnp.float32), axis=-1)
            w, sel = jax.lax.top_k(probs, K)
            w = w / jnp.sum(w, axis=-1, keepdims=True)
            w = w.astype(x.dtype)
            eid = sel.reshape(-1)
            tok = jnp.repeat(jnp.arange(T), K)
            oh = jax.nn.one_hot(eid, E, dtype=jnp.int32)
            pos = jnp.sum(jnp.cumsum(oh, axis=0) * oh, axis=-1) - 1
            valid = pos < CAP
            slot = jnp.where(valid, pos, CAP)
            xin = jnp.zeros((E, CAP + 1, Hd), x.dtype).at[eid, slot].set(x[tok])
            inp = xin[:, :CAP]
            h = jax.nn.silu(jnp.einsum('ech,ehi->eci', inp, wg)) * jnp.einsum('ech,ehi->eci', inp, wu)
            out = jnp.einsum('eci,eih->ech', h, wd)
            out_pad = jnp.concatenate([out, jnp.zeros((E, 1, Hd), out.dtype)], axis=1)
            g = out_pad[eid, slot] * (w.reshape(-1) * valid.astype(w.dtype))[:, None]
            y = jnp.zeros((T, Hd), x.dtype).at[tok].add(g)
            return y.reshape(B, S, Hd)
        key = jax.random.key(seed)
        k1, k2, k3, k4, k5 = jax.random.split(key, 5)
        hidden_states = jax.random.normal(k1, (1, 256, H), dtype=jnp.float32)
        gate_w = jax.random.normal(k2, (E, H), dtype=jnp.float32) * 0.02
        wg = jax.random.normal(k3, (E, H, I), dtype=jnp.float32) * 0.02
        wu = jax.random.normal(k4, (E, H, I), dtype=jnp.float32) * 0.02
        wd = jax.random.normal(k5, (E, I, H), dtype=jnp.float32) * 0.02
        return {'hidden_states': hidden_states, 'gate_w': gate_w, 'wg': wg, 'wu': wu, 'wd': wd}
    _L1_ffn_all = _L1_ffn_setup()
    _L1_ffn_in = {k: v for k, v in _L1_ffn_all.items() if k in ('gate_w', 'wg', 'wu', 'wd')}
    del _L1_ffn_all
    return {'x': x, 'ctx_1024': ctx_1024, 'fside_BxSx2_0': fside_BxSx2_0, 'L0_xattn_Wq': _L0_xattn_in['Wq'], 'L0_xattn_Wkv': _L0_xattn_in['Wkv'], 'L0_xattn_Wout': _L0_xattn_in['Wout'], 'L0_xattn_bout': _L0_xattn_in['bout'], 'L0_ffn_w_r': _L0_ffn_in['w_r'], 'L0_ffn_b_r': _L0_ffn_in['b_r'], 'L0_ffn_w1': _L0_ffn_in['w1'], 'L0_ffn_b1': _L0_ffn_in['b1'], 'L0_ffn_w2': _L0_ffn_in['w2'], 'L0_ffn_b2': _L0_ffn_in['b2'], 'L1_xattn_Wq': _L1_xattn_in['Wq'], 'L1_xattn_bq': _L1_xattn_in['bq'], 'L1_xattn_Wk': _L1_xattn_in['Wk'], 'L1_xattn_bk': _L1_xattn_in['bk'], 'L1_xattn_Wv': _L1_xattn_in['Wv'], 'L1_xattn_bv': _L1_xattn_in['bv'], 'L1_xattn_Wkv_dca': _L1_xattn_in['Wkv_dca'], 'L1_xattn_bkv_dca': _L1_xattn_in['bkv_dca'], 'L1_xattn_qn_w': _L1_xattn_in['qn_w'], 'L1_xattn_qn_b': _L1_xattn_in['qn_b'], 'L1_xattn_kn_w': _L1_xattn_in['kn_w'], 'L1_xattn_kn_b': _L1_xattn_in['kn_b'], 'L1_xattn_kn_dca_w': _L1_xattn_in['kn_dca_w'], 'L1_xattn_kn_dca_b': _L1_xattn_in['kn_dca_b'], 'L1_xattn_Wo': _L1_xattn_in['Wo'], 'L1_xattn_bo': _L1_xattn_in['bo'], 'L1_ffn_gate_w': _L1_ffn_in['gate_w'], 'L1_ffn_wg': _L1_ffn_in['wg'], 'L1_ffn_wu': _L1_ffn_in['wu'], 'L1_ffn_wd': _L1_ffn_in['wd']}

def reference(x, ctx_1024, fside_BxSx2_0, L0_xattn_Wq, L0_xattn_Wkv, L0_xattn_Wout, L0_xattn_bout, L0_ffn_w_r, L0_ffn_b_r, L0_ffn_w1, L0_ffn_b1, L0_ffn_w2, L0_ffn_b2, L1_xattn_Wq, L1_xattn_bq, L1_xattn_Wk, L1_xattn_bk, L1_xattn_Wv, L1_xattn_bv, L1_xattn_Wkv_dca, L1_xattn_bkv_dca, L1_xattn_qn_w, L1_xattn_qn_b, L1_xattn_kn_w, L1_xattn_kn_b, L1_xattn_kn_dca_w, L1_xattn_kn_dca_b, L1_xattn_Wo, L1_xattn_bo, L1_ffn_gate_w, L1_ffn_wg, L1_ffn_wu, L1_ffn_wd):
    import jax
    import jax.numpy as jnp

    def _L0_xattn_ref(x, ctx, pos_map, ctx_pos_map, Wq, Wkv, Wout, bout):
        import jax, jax.numpy as jnp
        import numpy as np
        DIM = 256
        CTX_DIM = 128
        N_HEADS = 32
        HEAD_DIM = DIM // N_HEADS
        POS_DIM = 2
        B, N, CTXN = (2, 256, 256)
        ROPE_BASE = 10000.0

        def apply_axial_rope(x, pos):
            b, n, h, d = x.shape
            p = pos.shape[-1]
            dpa = d // p
            half = dpa // 2
            freqs = ROPE_BASE ** (-jnp.arange(half, dtype=x.dtype) / half)
            ang = pos[..., :, None] * freqs
            cos = jnp.cos(ang)[:, :, None, :, :]
            sin = jnp.sin(ang)[:, :, None, :, :]
            xr = x.reshape(b, n, h, p, half, 2)
            x1, x2 = (xr[..., 0], xr[..., 1])
            out = jnp.stack([x1 * cos - x2 * sin, x1 * sin + x2 * cos], axis=-1)
            return out.reshape(b, n, h, d)
        b, n, _ = x.shape
        ctx_n = ctx.shape[1]
        q = (x @ Wq).reshape(b, n, N_HEADS, HEAD_DIM)
        k, v = jnp.split(ctx @ Wkv, 2, axis=-1)
        k = k.reshape(b, ctx_n, N_HEADS, HEAD_DIM)
        v = v.reshape(b, ctx_n, N_HEADS, HEAD_DIM)
        q = apply_axial_rope(q, pos_map)
        k = apply_axial_rope(k, ctx_pos_map)
        scale = 1.0 / np.sqrt(HEAD_DIM).astype(np.float32)
        logits = jnp.einsum('bqhd,bkhd->bhqk', q, k) * scale
        w = jax.nn.softmax(logits, axis=-1)
        attn = jnp.einsum('bhqk,bkhd->bqhd', w, v)
        attn = attn.reshape(b, n, N_HEADS * HEAD_DIM)
        return attn @ Wout + bout

    def _L0_ffn_ref(x, w_r, b_r, w1, b1, w2, b2):
        import jax, jax.numpy as jnp
        import numpy as np
        B, L, D = (4, 512, 256)
        DF = 4 * D
        CAPACITY_RATIO = 0.5
        b, l, d = x.shape
        k = int(l * CAPACITY_RATIO)
        scores = jnp.einsum('bld,d->bl', x, w_r) + b_r
        _, idx = jax.lax.top_k(scores, k)
        x_sel = jnp.take_along_axis(x, idx[:, :, None], axis=1)
        h = jax.nn.gelu(jnp.einsum('bkd,df->bkf', x_sel, w1) + b1)
        out_sel = jnp.einsum('bkf,fd->bkd', h, w2) + b2
        batch_ix = jnp.arange(b)[:, None]
        out = jnp.zeros_like(x).at[batch_ix, idx].set(out_sel)
        return out

    def _L1_xattn_ref(x, y, Wq, bq, Wk, bk, Wv, bv, Wkv_dca, bkv_dca, qn_w, qn_b, kn_w, kn_b, kn_dca_w, kn_dca_b, Wo, bo):
        import jax, jax.numpy as jnp
        import numpy as np
        B, S1, S2, DCA = (2, 256, 128, 16)
        QDIM, KDIM, H = (256, 128, 16)
        HD = QDIM // H
        SCALE = HD ** (-0.5)
        EPS = 1e-06
        DCA_WEIGHT = 1.0

        def _ln(t, w, b):
            m = jnp.mean(t, axis=-1, keepdims=True)
            v = jnp.var(t, axis=-1, keepdims=True)
            return (t - m) * jax.lax.rsqrt(v + EPS) * w + b

        def _attn(q, k, v):
            s = jnp.einsum('bhqd,bhkd->bhqk', q, k) * SCALE
            p = jax.nn.softmax(s, axis=-1)
            return jnp.einsum('bhqk,bhkd->bhqd', p, v)
        b, s1, _ = x.shape
        y_dca = y[:, -DCA:, :]
        y_main = y[:, :-DCA, :]
        kv_dca = (y_dca @ Wkv_dca + bkv_dca).reshape(b, DCA, 2, H, HD)
        k_dca = _ln(kv_dca[:, :, 0], kn_dca_w, kn_dca_b)
        v_dca = kv_dca[:, :, 1]
        s2 = y_main.shape[1]
        q = _ln((x @ Wq + bq).reshape(b, s1, H, HD), qn_w, qn_b)
        kv = jnp.concatenate([y_main @ Wk + bk, y_main @ Wv + bv], axis=-1)
        kv = kv.reshape(b, s2, H, 2 * HD)
        k = _ln(kv[..., :HD], kn_w, kn_b)
        v = kv[..., HD:]
        qT = q.transpose(0, 2, 1, 3)
        ctx = _attn(qT, k.transpose(0, 2, 1, 3), v.transpose(0, 2, 1, 3))
        ctx = ctx.transpose(0, 2, 1, 3).reshape(b, s1, QDIM)
        ctx_dca = _attn(qT, k_dca.transpose(0, 2, 1, 3), v_dca.transpose(0, 2, 1, 3))
        ctx_dca = ctx_dca.transpose(0, 2, 1, 3).reshape(b, s1, QDIM)
        ctx = ctx + DCA_WEIGHT * ctx_dca
        return ctx @ Wo + bo

    def _L1_ffn_ref(hidden_states, gate_w, wg, wu, wd):
        import jax, jax.numpy as jnp
        import numpy as np
        E = 64
        K = 8
        H = 256
        I = 96
        CAP = 64

        def _moe(hidden_states, gate_w, wg, wu, wd):
            B, S, Hd = hidden_states.shape
            x = hidden_states.reshape(-1, Hd)
            T = x.shape[0]
            logits = x @ gate_w.T
            probs = jax.nn.softmax(logits.astype(jnp.float32), axis=-1)
            w, sel = jax.lax.top_k(probs, K)
            w = w / jnp.sum(w, axis=-1, keepdims=True)
            w = w.astype(x.dtype)
            eid = sel.reshape(-1)
            tok = jnp.repeat(jnp.arange(T), K)
            oh = jax.nn.one_hot(eid, E, dtype=jnp.int32)
            pos = jnp.sum(jnp.cumsum(oh, axis=0) * oh, axis=-1) - 1
            valid = pos < CAP
            slot = jnp.where(valid, pos, CAP)
            xin = jnp.zeros((E, CAP + 1, Hd), x.dtype).at[eid, slot].set(x[tok])
            inp = xin[:, :CAP]
            h = jax.nn.silu(jnp.einsum('ech,ehi->eci', inp, wg)) * jnp.einsum('ech,ehi->eci', inp, wu)
            out = jnp.einsum('eci,eih->ech', h, wd)
            out_pad = jnp.concatenate([out, jnp.zeros((E, 1, Hd), out.dtype)], axis=1)
            g = out_pad[eid, slot] * (w.reshape(-1) * valid.astype(w.dtype))[:, None]
            y = jnp.zeros((T, Hd), x.dtype).at[tok].add(g)
            return y.reshape(B, S, Hd)
        return _moe(hidden_states, gate_w, wg, wu, wd)
    x = x + _L0_xattn_ref(_layernorm(x, axis=-1), ctx_1024, fside_BxSx2_0, fside_BxSx2_0, L0_xattn_Wq, L0_xattn_Wkv, L0_xattn_Wout, L0_xattn_bout)
    x = x + _L0_ffn_ref(_layernorm(x, axis=-1), L0_ffn_w_r, L0_ffn_b_r, L0_ffn_w1, L0_ffn_b1, L0_ffn_w2, L0_ffn_b2)
    x = x + _L1_xattn_ref(_layernorm(x, axis=-1), ctx_1024, L1_xattn_Wq, L1_xattn_bq, L1_xattn_Wk, L1_xattn_bk, L1_xattn_Wv, L1_xattn_bv, L1_xattn_Wkv_dca, L1_xattn_bkv_dca, L1_xattn_qn_w, L1_xattn_qn_b, L1_xattn_kn_w, L1_xattn_kn_b, L1_xattn_kn_dca_w, L1_xattn_kn_dca_b, L1_xattn_Wo, L1_xattn_bo)
    x = x + _L1_ffn_ref(_layernorm(x, axis=-1), L1_ffn_gate_w, L1_ffn_wg, L1_ffn_wu, L1_ffn_wd)
    return x

_drawn_inputs = setup_inputs


def setup_inputs(seed=0):
    import zlib

    import numpy as np

    out = dict(_drawn_inputs(seed))
    spreads = {'L0_xattn_bout': (0.0, 0.1),
     'L0_ffn_b1': (0.0, 0.38),
     'L0_ffn_b2': (0.0, 0.1),
     'L1_xattn_bq': (0.0, 0.8),
     'L1_xattn_bk': (0.0, 0.399),
     'L1_xattn_bv': (0.0, 0.429),
     'L1_xattn_bkv_dca': (0.0, 0.27),
     'L1_xattn_qn_w': (1.0, 0.6),
     'L1_xattn_qn_b': (0.0, 0.8),
     'L1_xattn_kn_w': (1.0, 0.6),
     'L1_xattn_kn_b': (0.0, 0.8),
     'L1_xattn_kn_dca_w': (1.0, 0.6),
     'L1_xattn_kn_dca_b': (0.0, 0.8),
     'L1_xattn_bo': (0.0, 0.1)}
    factors = {'L1_xattn_Wq': 2.797,
     'L1_ffn_gate_w': 8.0,
     'L1_ffn_wg': 8.0,
     'L1_ffn_wu': 8.0,
     'L1_ffn_wd': 8.0}
    for name, (base, spread) in spreads.items():
        noise = np.random.default_rng([zlib.crc32(name.encode()), seed]).standard_normal(out[name].shape)
        drawn = base * np.exp(spread * noise) if base else spread * noise
        out[name] = jnp.asarray(drawn.astype(out[name].dtype))
    for name, factor in factors.items():
        out[name] = (out[name] * factor).astype(out[name].dtype)
    return out
```

```python
from contextlib import ExitStack

import numpy as np
import concourse.bass as bass
import concourse.mybir as mybir

F32 = mybir.dt.float32
U32 = mybir.dt.uint32
ALU = mybir.AluOpType
ACT = mybir.ActivationFunctionType
AX = mybir.AxisListType

P = 128
B, S, D = 64, 64, 256
C = 128
T = B * S
NT = T // P
KC = D // P
BANK = 512
LN_EPS = 1e-5

H0, HD0 = 32, 8
G0 = 4
HG0 = H0 // G0
NHP0 = H0 // 2
VW0 = 2 * HD0 + 2
ROPE_BASE = 10000.0
TWO_PI = 2.0 * np.pi
ROUND = 12582912.0

F = 1024
FC = F // P
KEEP = S // 2
NQ = NT // 2

H1, HD1 = 16, 16
DCA = 16
MAIN = S - DCA
HG1 = H1 // KC
NHP1 = H1 // 2
NHC1 = NHP1 // KC
VW1 = 2 * 2 * HD1 + 4
HEAD_EPS = 1e-6

E, TOPK, I, CAP = 64, 8, 96, 64
NP_E = E // 2
ROW = D + E
TAKEN = -3.0e38


def pipelined(eng, step, tiles, depth):
    first = depth + depth % 2

    def peeled(n):
        step(n, n // 2, n % 2, [0 <= n - k < tiles for k in range(depth)])

    for n in range(first):
        peeled(n)
    with eng.Fori(first // 2, tiles // 2) as i:
        for u in range(2):
            step(2 * i + u, i, u, [True] * depth)
    for n in range(tiles, tiles + depth - 1):
        peeled(n)


def later(t, n):
    return not isinstance(t, int) or t >= n


def tile_of(buf, t):
    return buf[:, t, :] if isinstance(t, int) else buf[:, bass.ds(t, 1), :].rearrange("p a d -> p (a d)")


def column_of(buf, t):
    return buf[:, t:t + 1] if isinstance(t, int) else buf[:, bass.ds(t, 1)]


def spread(ap, n):
    return ap.rearrange("p (a k) -> p a k", a=1).to_broadcast([ap.shape[0], n, ap.shape[1]])


def stretch(ap, n):
    return ap.rearrange("p (h a) -> p h a", a=1).to_broadcast([ap.shape[0], ap.shape[1], n])


def row_statistics(dve, k, done):
    mean_e, mean_o = k.raw[:, :, 1], k.raw[:, :, 4]
    dve.tensor_tensor(k.mean2[:, :], mean_e, mean_o, ALU.add).then_inc(done, 1)
    dve.tensor_tensor(k.apart[:, :], mean_e, mean_o, ALU.subtract).then_inc(done, 1)
    dve.tensor_tensor(k.square[:, :], k.raw[:, :, 2], k.raw[:, :, 5], ALU.add).then_inc(done, 1)
    dve.wait_ge(done, 2)
    dve.scalar_tensor_tensor(out=k.spread2[:, :], in0=k.apart[:, :], scalar=0.25, in1=k.apart[:, :],
                             op0=ALU.mult, op1=ALU.mult).then_inc(done, 1)
    dve.wait_ge(done, 4)
    dve.scalar_tensor_tensor(out=k.var[:, :], in0=k.square[:, :], scalar=1.0 / D, in1=k.spread2[:, :],
                             op0=ALU.mult, op1=ALU.add).then_inc(done, 1)


def row_scales(act, k, statistics_done, ln_done, scale_done):
    act.wait_ge(statistics_done, 5)
    act.activation(k.lnv[:, :], k.var[:, :], ACT.Ln, bias=k.ln_eps[:, 0:1]).then_inc(ln_done, 1)
    act.wait_ge(ln_done, 1)
    act.activation(k.rstd[:, :], k.lnv[:, :], ACT.Exp, scale=-0.5).then_inc(scale_done, 1)


def row_shifts(dve, k, scale_done, shift_done):
    dve.wait_ge(scale_done, 1)
    dve.scalar_tensor_tensor(out=k.nmr[:, :], in0=k.mean2[:, :], scalar=-0.5, in1=k.rstd[:, :],
                             op0=ALU.mult, op1=ALU.mult).then_inc(shift_done, 1)
    dve.wait_ge(shift_done, 1)


class Shared:
    pass


class Scope:

    def __init__(self, nc, stack):
        self.nc, self.stack = nc, stack
        self.signals = []

    def sb(self, name, shape, dt=F32):
        return self.stack.enter_context(self.nc.sbuf_tensor(name, shape, dt))

    def sems(self, names):
        self.signals = [self.nc.alloc_semaphore(name=n) for n in names.split()]
        return self.signals

    def end(self):
        self.nc.clear_and_free_semaphores(self.signals)
        self.nc.all_engine_barrier()


def first_attention(nc, ins, k, bank):
    with ExitStack() as stack:
        z = Scope(nc, stack)
        cos_t = z.sb("cos_t", [P, NT, S])
        sin_t = z.sb("sin_t", [P, NT, S])
        freq4 = z.sb("freq4", [4, P])
        sign = z.sb("sign", [P, 1])
        head_mask = z.sb("head_mask", [P, HG0])
        pos4 = z.sb("pos4", [4, NT * S])
        ang = z.sb("ang", [P, 2, BANK])
        wq, wq_sw = z.sb("wq", [P, KC, D]), z.sb("wq_sw", [P, KC, D])
        wk, wk_sw, wv = z.sb("wk", [P, D]), z.sb("wk_sw", [P, D]), z.sb("wv", [P, D])
        wo = z.sb("wo", [P, KC, D])
        bo = z.sb("bo", [P, D])
        ctx_t = z.sb("ctx_t", [P, 2, P])
        xn = z.sb("xn", [P, 2, D])
        xn_t = z.sb("xn_t", [P, 2, KC, P])
        part_a, part_b = z.sb("part_a", [P, 2, BANK]), z.sb("part_b", [P, 2, BANK])
        k_rot = z.sb("k_rot", [P, 2, G0, S])
        q_bd = z.sb("q_bd", [P, 2, G0, 2, S])
        k_bd = z.sb("k_bd", [P, 2, G0, HG0, S])
        top = z.sb("top", [P, 2, HG0])
        sub = z.sb("sub", [P, 2, BANK])
        pr_t = z.sb("pr_t", [P, G0, 4, P])
        v_bd = z.sb("v_bd", [P, 2, 2, NHP0, VW0])
        rcp = z.sb("rcp", [P, H0])
        att = z.sb("att", [P, 2, D])
        att_t = z.sb("att_t", [P, 2, KC, P])

        (a_const, a_weights, a_xin0, a_xin1, a_xin2, a_xin3, a_ctx0, a_ctx1, a_fill, a_ang, a_turns, a_whole,
         a_wrapped, a_neg, a_mirror, a_sin, a_cos, a_raw, a_stats, a_lnv_done, a_rstd_done, a_nmr_done, a_xn,
         a_xnT, a_xnTc, a_q, a_k, a_v, a_ropeq, a_ropek, a_qbd, a_krot, a_kbd, a_vbd, a_s, a_top, a_sub,
         a_prT, a_exp, a_pv, a_rcp, a_att, a_attT, a_attTc, a_out, a_bias, a_x1, a_raw1
         ) = z.sems(
             "a_const a_weights a_xin0 a_xin1 a_xin2 a_xin3 a_ctx0 a_ctx1 a_fill a_ang a_turns a_whole a_wrapped "
             "a_neg a_mirror a_sin a_cos a_raw a_stats a_lnv_done a_rstd_done a_nmr_done a_xn a_xnT a_xnTc a_q a_k "
             "a_v a_ropeq a_ropek a_qbd a_krot a_kbd a_vbd a_s a_top a_sub a_prT a_exp a_pv a_rcp a_att a_attT "
             "a_attTc a_out a_bias a_x1 a_raw1")
        x_in, ctx_in = [a_xin0, a_xin1, a_xin2, a_xin3], [a_ctx0, a_ctx1]

        b_turn, b_q, b_k, b_v, b_s, b_pr, b_o = bank[0], bank[1], bank[2], bank[3], bank[4:6], bank[6], bank[7]
        NANG = NT * S // BANK

        consts = [(k.ident[:, :], ins["ident"]), (freq4[:, :], ins["freq4"]), (sign[:, :], ins["rope_sign"]),
                  (head_mask[:, :], ins["head_mask0"]), (pos4[:, :], ins["pos4"])]
        weights = [(wk[:, :], ins["L0_xattn_Wkv"][:, 0:D]),
                   (wk_sw[:, :], ins["wk_swapped"]),
                   (wq[:, :, :], ins["L0_xattn_Wq"].rearrange("(c p) n -> p c n", p=P)),
                   (wq_sw[:, :, :], ins["wq_swapped"].rearrange("(c p) n -> p c n", p=P)),
                   (wv[:, :], ins["L0_xattn_Wkv"][:, D:2 * D]),
                   (wo[:, :, :], ins["L0_xattn_Wout"].rearrange("(c p) n -> p c n", p=P)),
                   (bo[:, :], over_rows(ins["L0_xattn_bout"]))]
        x_rows = ins["x"].rearrange("(t b) s d -> (b s) t d", b=2)

        inner = stack.enter_context(ExitStack())
        block = inner.enter_context(nc.Block())

        @block.sync
        def _(sp):
            for dst, src in consts:
                sp.dma_start(dst, src).then_inc(a_const, 16)

            def load(t, i, u):
                if later(t, 2):
                    sp.wait_ge(ctx_in[u], 16 * i)
                    sp.wait_ge(a_v, t - 1)
                    sp.wait_ge(a_k, t - 1)
                sp.dma_start(ctx_t[:, u, :], ins["ctx_t"][:, bass.ds(t * P, P)]).then_inc(ctx_in[u], 16)

            for c, part_in in enumerate(x_in):
                part = slice(c * NT // len(x_in), (c + 1) * NT // len(x_in))
                sp.dma_start(k.xres[:, part, :], x_rows[:, part, :]).then_inc(part_in, 16)
            load(0, 0, 0)
            load(1, 0, 1)
            for dst, src in weights:
                sp.dma_start(dst, src).then_inc(a_weights, 16)
            with sp.Fori(1, NT // 2) as i:
                for u in range(2):
                    load(2 * i + u, i, u)

        @block.gpsimd
        def _(pool):
            for dst, src in k.later_loads:
                pool.dma_start(dst, src).then_inc(k.loaded, 16)
            pool.memset(q_bd[:, :, :, :, :], 0.0).then_inc(a_fill, 1)
            pool.memset(v_bd[:, :, :, :, :], 0.0).then_inc(a_fill, 1)
            pool.memset(k.ln_eps[:, :], LN_EPS).then_inc(a_fill, 1)
            pool.wait_ge(a_fill, 3)
            for h in range(2):
                pool.memset(v_bd[64 * h:64 * h + 64, :, :, :, 2 * HD0 + h:2 * HD0 + h + 1], 1.0).then_inc(a_fill, 1)
            pool.wait_ge(a_const, 16 * len(consts))
            pool.wait_ge(a_weights, 16 * len(weights))

            def step(n, i, u, on):
                if on[0]:
                    t = n
                    pool.wait_ge(a_xn, t + 1)
                    pool.tensor_tensor(tile_of(k.xres, t), tile_of(k.xres, t), bo[:, :], ALU.add).then_inc(a_bias, 1)
                    pool.wait_ge(a_krot, t + 1)
                    if later(t, 2):
                        pool.wait_ge(a_s, G0 * (t - 1))
                    for g in range(G0):
                        pool.tensor_tensor(k_bd[:, u, g, :, :], spread(k_rot[:, u, g, :], HG0),
                                           stretch(head_mask[:, :], S), ALU.mult).then_inc(a_kbd, 1)
            pipelined(pool, step, NT, 4)

        @block.tensor
        def _(pe):
            pe.wait_ge(a_const, 16 * len(consts))
            for c in range(NANG):
                if c >= 2:
                    pe.wait_ge(a_wrapped, c - 1)
                pe.matmul(bank[c % 2][:, :], freq4[:, :], pos4[:, c * BANK:(c + 1) * BANK],
                          start=True, stop=True).then_inc(a_ang, 1)
            pe.wait_ge(a_weights, 16 * len(weights))
            pe.wait_ge(a_wrapped, NANG)

            def scores(t, u, g):
                if g == 0:
                    pe.wait_ge(a_qbd, 2 * t + 2)
                pe.wait_ge(a_kbd, G0 * t + g + 1)
                if later(t, 1) or g >= 2:
                    pe.wait_ge(a_sub, G0 * t + g - 1)
                pe.matmul(b_s[g % 2][:, :], q_bd[:, u, g, :, :].rearrange("p b s -> p (b s)"),
                          k_bd[:, u, g, :, :].rearrange("p h k -> p (h k)"), start=True, stop=True).then_inc(a_s, 1)

            def turn(t, g):
                pe.wait_ge(a_sub, G0 * t + g + 1)
                if later(t, 1) or g >= 1:
                    pe.wait_ge(a_exp, G0 * t + g)
                for j in range(4):
                    m = pe.transpose(b_pr[:, j * P:(j + 1) * P], sub[:, g % 2, j * P:(j + 1) * P], k.ident[:, :])
                m.then_inc(a_prT, 1)

            def values(t, u, g):
                pe.wait_ge(a_exp, G0 * t + g + 1)
                if g == 0:
                    pe.wait_ge(a_vbd, 2 * t + 2)
                    if later(t, 1):
                        pe.wait_ge(a_att, t)
                for j in range(4):
                    hp = 4 * g + j
                    for b in range(2):
                        m = pe.matmul(b_o[64 * b:64 * b + 64, hp * VW0:(hp + 1) * VW0], pr_t[:, g, j, b * S:(b + 1) * S],
                                      v_bd[:, u, b, hp, :], start=True, stop=True)
                m.then_inc(a_pv, 1)

            def project(bnk, w2, rhs, chunks):
                for n, w in enumerate(w2):
                    for g in range(G0):
                        for c in range(chunks):
                            for b in range(2):
                                m = pe.matmul(bnk[64 * b:64 * b + 64, n * D + g * S:n * D + (g + 1) * S],
                                              w(c, g), rhs(c, b), start=(c == 0), stop=(c == chunks - 1))
                return m

            def step(n, i, u, on):
                t, tv, a, f = n, n - 1, n - 2, n - 3
                v = 1 - u
                if on[2]:
                    scores(a, u, 0)
                    scores(a, u, 1)
                if on[3]:
                    pe.wait_ge(a_att, f + 1)
                    if later(f, 1):
                        pe.wait_ge(a_x1, f)
                    pe.wait_ge(a_xnTc, n if on[0] else NT)
                    for c in range(KC):
                        m = pe.transpose(b_turn[:, c * P:(c + 1) * P], att[:, v, c * P:(c + 1) * P], k.ident[:, :])
                    m.then_inc(a_attT, 1)
                if on[0]:
                    pe.wait_ge(ctx_in[u], 16 * (i + 1))
                    if later(t, 1):
                        pe.wait_ge(a_ropek, 2 * t)
                    project(b_k, [lambda c, g: wk[:, g * 64:(g + 1) * 64], lambda c, g: wk_sw[:, g * 64:(g + 1) * 64]],
                            lambda c, b: ctx_t[:, u, b * S:(b + 1) * S], 1).then_inc(a_k, 1)
                if on[2]:
                    turn(a, 0)
                    scores(a, u, 2)
                if on[3]:
                    pe.wait_ge(a_attTc, f + 1)
                    for c in range(KC):
                        m = pe.matmul(b_turn[:, D:2 * D], att_t[:, v, c, :], wo[:, c, :], start=(c == 0), stop=(c == KC - 1))
                    m.then_inc(a_out, 1)
                if on[1]:
                    if later(tv, 1):
                        pe.wait_ge(a_vbd, 2 * tv)
                    for b in range(2):
                        for h in range(2):
                            m = pe.matmul(b_v[64 * h:64 * h + 64, b * D:(b + 1) * D], ctx_t[:, v, b * S:(b + 1) * S],
                                          wv[:, :], start=True, stop=True)
                    m.then_inc(a_v, 1)
                if on[2]:
                    turn(a, 1)
                    values(a, u, 0)
                    scores(a, u, 3)
                if on[0]:
                    pe.wait_ge(a_xn, t + 1)
                    if on[3]:
                        pe.wait_ge(a_x1, f + 1)
                    for c in range(KC):
                        m = pe.transpose(b_turn[:, c * P:(c + 1) * P], xn[:, u, c * P:(c + 1) * P], k.ident[:, :])
                    m.then_inc(a_xnT, 1)
                if on[2]:
                    turn(a, 2)
                    values(a, u, 1)
                if on[0]:
                    pe.wait_ge(a_xnTc, t + 1)
                    if later(t, 1):
                        pe.wait_ge(a_ropeq, 2 * t)
                    project(b_q, [lambda c, g: wq[:, c, g * 64:(g + 1) * 64], lambda c, g: wq_sw[:, c, g * 64:(g + 1) * 64]],
                            lambda c, b: xn_t[:, u, c, b * S:(b + 1) * S], KC).then_inc(a_q, 1)
                if on[2]:
                    turn(a, 3)
                    values(a, u, 2)
                    values(a, u, 3)
            pipelined(pe, step, NT, 4)

        @block.scalar
        def _(act):
            act.wait_ge(a_const, 16 * len(consts))
            for c in range(NANG):
                tiles = slice(c * BANK // S, (c + 1) * BANK // S)
                act.wait_ge(a_wrapped, c + 1)
                act.activation(sin_t[:, tiles, :].rearrange("p t s -> p (t s)"), ang[:, c % 2, :], ACT.Sin,
                               scale=sign[:, 0:1]).then_inc(a_sin, 1)
                act.wait_ge(a_mirror, c + 1)
                act.activation(cos_t[:, tiles, :].rearrange("p t s -> p (t s)"), part_a[:, c % 2, :],
                               ACT.Sin).then_inc(a_cos, 1)
            act.preload_act_table_set("natural_log_exp_and_others")
            act.wait_ge(a_fill, 5)
            row_scales(act, k, a_stats, a_lnv_done, a_rstd_done)

            def step(n, i, u, on):
                t, tv, a, f = n, n - 1, n - 2, n - 3
                v = 1 - u
                def exps(g):
                    act.wait_ge(a_prT, G0 * a + g + 1)
                    if later(a, 1):
                        act.wait_ge(a_pv, G0 * (a - 1) + g + 1)
                    act.activation(pr_t[:, g, :, :].rearrange("p j q -> p (j q)"), b_pr[:, :], ACT.Exp).then_inc(a_exp, 1)

                if on[3]:
                    act.wait_ge(a_attT, f + 1)
                    act.activation(att_t[:, v, :, :].rearrange("p c q -> p (c q)"), b_turn[:, 0:D],
                                   ACT.Copy).then_inc(a_attTc, 1)
                if on[2]:
                    exps(0)
                if on[1]:
                    act.wait_ge(a_v, tv + 1)
                    if later(tv, 2):
                        act.wait_ge(a_pv, G0 * (tv - 1))
                    vp = b_v[:, :].rearrange("p (b n h d) -> p b n h d", b=2, n=NHP0, h=2)
                    for h in range(2):
                        act.activation(v_bd[64 * h:64 * h + 64, v, :, :, h * HD0:(h + 1) * HD0],
                                       vp[64 * h:64 * h + 64, :, :, h, :], ACT.Copy).then_inc(a_vbd, 1)
                if on[2]:
                    exps(1)
                if on[0]:
                    act.wait_ge(a_xnT, t + 1)
                    act.activation(xn_t[:, u, :, :].rearrange("p c q -> p (c q)"), b_turn[:, 0:D],
                                   ACT.Copy).then_inc(a_xnTc, 1)
                if on[2]:
                    exps(2)
                    exps(3)
            pipelined(act, step, NT, 4)

        @block.vector
        def _(dve):
            for c in range(NANG):
                whole, angle, mirror = part_b[:, c % 2, :], ang[:, c % 2, :], part_a[:, c % 2, :]
                dve.wait_ge(a_ang, c + 1)
                dve.tensor_scalar(whole, bank[c % 2][:, :], 1.0 / TWO_PI, ROUND, ALU.mult, ALU.add).then_inc(a_turns, 1)
                dve.wait_ge(a_turns, c + 1)
                dve.tensor_scalar(whole, whole, ROUND, -TWO_PI, ALU.subtract, ALU.mult).then_inc(a_whole, 1)
                dve.wait_ge(a_whole, c + 1)
                if c >= 2:
                    dve.wait_ge(a_sin, c - 1)
                    dve.wait_ge(a_cos, c - 1)
                dve.tensor_tensor(angle, bank[c % 2][:, :], whole, ALU.add).then_inc(a_wrapped, 1)
                dve.wait_ge(a_wrapped, c + 1)
                dve.scalar_tensor_tensor(out=mirror, in0=angle, scalar=-1.0, in1=angle,
                                         op0=ALU.mult, op1=ALU.min).then_inc(a_neg, 1)
                dve.wait_ge(a_neg, c + 1)
                dve.tensor_scalar(mirror, mirror, float(np.pi / 2), None, ALU.add).then_inc(a_mirror, 1)
            dve.wait_ge(a_sin, NANG)
            dve.wait_ge(a_cos, NANG)
            dve.wait_ge(a_fill, 5)
            for c, part_in in enumerate(x_in):
                dve.wait_ge(part_in, 16)
                with dve.Fori(c * NT // len(x_in), (c + 1) * NT // len(x_in)) as t:
                    dve.bn_stats(tile_of(k.raw, t), tile_of(k.xres, t)).then_inc(a_raw, 1)
            dve.wait_ge(a_raw, NT)
            row_statistics(dve, k, a_stats)
            row_shifts(dve, k, a_rstd_done, a_nmr_done)

            def step(n, i, u, on):
                t, a, f = n, n - 2, n - 3
                v = 1 - u

                def softmax_part(g):
                    sc = b_s[g % 2][:, :].rearrange("p (h k) -> p h k", k=S)
                    dve.wait_ge(a_s, G0 * a + g + 1)
                    dve.tensor_reduce(top[:, g % 2, :], sc, AX.X, ALU.max).then_inc(a_top, 1)
                    dve.wait_ge(a_top, G0 * a + g + 1)
                    if later(a, 1) or g >= 2:
                        dve.wait_ge(a_prT, G0 * a + g - 1)
                    dve.tensor_tensor(sub[:, g % 2, :].rearrange("p (h k) -> p h k", k=S), sc,
                                      stretch(top[:, g % 2, :], S), ALU.subtract).then_inc(a_sub, 1)

                def rope(done, bnk, o):
                    pa, pb = part_a[:, o, 0:D], part_b[:, o, 0:D]
                    for dst, src, table in ((pa, bnk[:, 0:D], cos_t), (pb, bnk[:, D:2 * D], sin_t)):
                        dve.tensor_tensor(dst.rearrange("p (g k) -> p g k", k=S), src.rearrange("p (g k) -> p g k", k=S),
                                          spread(tile_of(table, t), G0), ALU.mult).then_inc(done, 1)
                    dve.wait_ge(done, 2 * t + 2)
                    return pa, pb

                if on[2]:
                    softmax_part(0)
                    softmax_part(1)
                if on[0]:
                    if later(t, 2):
                        dve.wait_ge(a_xnT, t - 1)
                    dve.tensor_scalar(xn[:, u, :], tile_of(k.xres, t), column_of(k.rstd, t), column_of(k.nmr, t),
                                      ALU.mult, ALU.add).then_inc(a_xn, 1)
                    dve.wait_ge(a_k, t + 1)
                    if later(t, 2):
                        dve.wait_ge(a_kbd, G0 * (t - 1))
                    pa, pb = rope(a_ropek, b_k, 1)
                    dve.tensor_tensor(k_rot[:, u, :, :].rearrange("p g k -> p (g k)"), pa, pb, ALU.add).then_inc(a_krot, 1)
                if on[3]:
                    dve.wait_ge(a_out, f + 1)
                    dve.wait_ge(a_bias, f + 1)
                    dve.tensor_tensor(tile_of(k.xres, f), b_turn[:, D:2 * D], tile_of(k.xres, f), ALU.add).then_inc(a_x1, 1)
                if on[2]:
                    softmax_part(2)
                if on[3]:
                    dve.wait_ge(a_x1, f + 1)
                if on[2]:
                    softmax_part(3)
                if on[3]:
                    dve.bn_stats(tile_of(k.raw, f), tile_of(k.xres, f)).then_inc(a_raw1, 1)
                if on[0]:
                    dve.wait_ge(a_q, t + 1)
                    pa, pb = rope(a_ropeq, b_q, 0)
                    if later(t, 2):
                        dve.wait_ge(a_s, G0 * (t - 1))
                    for b in range(2):
                        rows = slice(64 * b, 64 * b + 64)
                        dve.tensor_tensor(q_bd[rows, u, :, b, :], pa[rows, :].rearrange("p (g k) -> p g k", k=S),
                                          pb[rows, :].rearrange("p (g k) -> p g k", k=S), ALU.add).then_inc(a_qbd, 1)
                if on[2]:
                    o3 = b_o[:, 0:NHP0 * VW0].rearrange("p (n w) -> p n w", w=VW0)
                    dve.wait_ge(a_pv, G0 * a + G0)
                    dve.reciprocal(rcp[:, :].rearrange("p (n h) -> p n h", h=2), o3[:, :, 2 * HD0:VW0]).then_inc(a_rcp, 1)
                    dve.wait_ge(a_rcp, a + 1)
                    if later(a, 2):
                        dve.wait_ge(a_attT, a - 1)
                    dve.tensor_tensor(att[:, u, :].rearrange("p (n h d) -> p n h d", n=NHP0, h=2),
                                      o3[:, :, 0:2 * HD0].rearrange("p n (h d) -> p n h d", h=2),
                                      rcp[:, :].rearrange("p (n h a) -> p n h a", h=2, a=1).to_broadcast([P, NHP0, 2, HD0]),
                                      ALU.mult).then_inc(a_att, 1)
            pipelined(dve, step, NT, 4)
            dve.wait_ge(a_raw1, NT)
        inner.close()
        z.end()


def kept_feed_forward(nc, ins, k, bank):
    with ExitStack() as stack:
        z = Scope(nc, stack)
        xn = z.sb("f_xn", [P, 2, 2, D])
        junk = z.sb("f_junk", [P, 2, D])
        junk2 = z.sb("f_junk2", [P, 2, P])
        score = z.sb("f_score", [P, 2, 2])
        above, tied = z.sb("f_above", [P, 2, 2]), z.sb("f_tied", [P, 2, 2])
        pick = z.sb("f_pick", [P, 2, 2, P])
        pick_t = z.sb("f_pick_t", [P, 2, 2, P])
        xs_t = z.sb("f_xs_t", [P, 2, KC, P])
        hid = z.sb("f_hid", [P, 2, FC, P])
        ys = z.sb("f_ys", [P, 2, D])
        (f_fill, f_stats, f_lnv_done, f_rstd_done, f_nmr_done, f_xn_done, f_score_done, f_row, f_above_done,
         f_tied_done, f_pick_done, f_xsT, f_xsTc, f_pickT, f_pickTc, f_h, f_gelu, f_y, f_ys_done, f_returned,
         f_x2, f_raw
         ) = z.sems(
             "f_fill f_stats f_lnv_done f_rstd_done f_nmr_done f_xn_done f_score_done f_row f_above_done "
             "f_tied_done f_pick_done f_xsT f_xsTc f_pickT f_pickTc f_h f_gelu f_y f_ys_done f_returned f_x2 f_raw")
        b_row, b_xs, b_pick, b_h, b_y, b_back = bank[0], bank[1], bank[2], bank[3:5], bank[5], bank[6]

        inner = stack.enter_context(ExitStack())
        block = inner.enter_context(nc.Block())

        @block.gpsimd
        def _(pool):
            pool.memset(pick[:, :, :, :], 0.0).then_inc(f_fill, 1)

        @block.tensor
        def _(pe):
            pe.wait_ge(k.loaded, 16 * len(k.later_loads))

            def step(n, i, u, on):
                q, m, f = n, n - 1, n - 2
                v = 1 - u
                if on[2]:
                    pe.wait_ge(f_ys_done, f + 1)
                    if later(f, 1):
                        pe.wait_ge(f_x2, 2 * f)
                    for j in range(2):
                        pe.matmul(b_back[:, j * D:(j + 1) * D], pick_t[:, u, j, :], ys[:, u, :],
                                  start=True, stop=True).then_inc(f_returned, 1)
                if on[0]:
                    for j in range(2):
                        pe.wait_ge(f_score_done, 2 * q + j + 1)
                        if later(q, 1):
                            pe.wait_ge(f_tied_done, 2 * q)
                        pe.transpose(b_row[:, j * P:(j + 1) * P], score[:, u, j:j + 1].to_broadcast([P, P]),
                                     k.ident[:, :]).then_inc(f_row, 1)
                if on[1]:
                    pe.wait_ge(f_xsTc, m + 1)
                    for c in range(FC):
                        if c % 4 == 0 and later(m, 1):
                            pe.wait_ge(f_gelu, FC * (m - 1) + c + 4)
                        for d in range(KC):
                            mm = pe.matmul(b_h[c // 4][:, (c % 4) * P:(c % 4 + 1) * P], k.w1[:, d, c * P:(c + 1) * P],
                                           xs_t[:, v, d, :], start=(d == 0), stop=(d == KC - 1))
                        mm.then_inc(f_h, 1)
                if on[0]:
                    if later(q, 1):
                        pe.wait_ge(f_xsTc, q)
                        pe.wait_ge(f_pickTc, q)
                    for j in range(2):
                        pe.wait_ge(f_pick_done, 2 * q + j + 1)
                        for c in range(KC):
                            mm = pe.matmul(b_xs[:, c * P + j * 64:c * P + j * 64 + 64], xn[:, u, j, c * P:(c + 1) * P],
                                           pick[:, u, j, j * 64:j * 64 + 64], start=True, stop=True)
                    mm.then_inc(f_xsT, 1)
                    for j in range(2):
                        mm = pe.transpose(b_pick[:, j * P:(j + 1) * P], pick[:, u, j, :], k.ident[:, :])
                    mm.then_inc(f_pickT, 1)
                if on[1]:
                    if later(m, 1):
                        pe.wait_ge(f_ys_done, m)
                    for c in range(FC):
                        pe.wait_ge(f_gelu, FC * m + c + 1)
                        mm = pe.matmul(b_y[:, 0:D], hid[:, v, c, :], k.w2[:, c, :], start=(c == 0), stop=(c == FC - 1))
                    mm.then_inc(f_y, 1)
            pipelined(pe, step, NQ, 3)

        @block.scalar
        def _(act):
            row_scales(act, k, f_stats, f_lnv_done, f_rstd_done)
            act.preload_act_table(ACT.Gelu_apprx_tanh)
            act.wait_ge(k.loaded, 16 * len(k.later_loads))

            def step(n, i, u, on):
                q, m = n, n - 1
                v = 1 - u
                if on[1]:
                    for c in range(FC):
                        act.wait_ge(f_h, FC * m + (c // 4) * 4 + 4)
                        if c == 0 and later(m, 2):
                            act.wait_ge(f_y, m - 1)
                        act.activation(hid[:, v, c, :], b_h[c // 4][:, (c % 4) * P:(c % 4 + 1) * P], ACT.Gelu_apprx_tanh,
                                       bias=k.b1[:, c:c + 1]).then_inc(f_gelu, 1)
                if on[0]:
                    act.wait_ge(f_xsT, q + 1)
                    if later(q, 2):
                        act.wait_ge(f_h, FC * (q - 1))
                    act.activation(xs_t[:, u, :, :].rearrange("p c s -> p (c s)"), b_xs[:, 0:KC * P],
                                   ACT.Copy).then_inc(f_xsTc, 1)
                    act.wait_ge(f_pickT, q + 1)
                    if later(q, 2):
                        act.wait_ge(f_returned, 2 * (q - 1))
                    act.activation(pick_t[:, u, :, :].rearrange("p j s -> p (j s)"), b_pick[:, 0:2 * P],
                                   ACT.Copy).then_inc(f_pickTc, 1)
            pipelined(act, step, NQ, 3)

        @block.vector
        def _(dve):
            row_statistics(dve, k, f_stats)
            row_shifts(dve, k, f_rstd_done, f_nmr_done)
            dve.wait_ge(f_fill, 1)
            dve.wait_ge(k.loaded, 16 * len(k.later_loads))

            def step(n, i, u, on):
                q, m, f = n, n - 1, n - 2
                v = 1 - u
                if on[0]:
                    for j in range(2):
                        t = 2 * q + j
                        if later(q, 2):
                            dve.wait_ge(f_xsT, q - 1)
                        dve.tensor_scalar(xn[:, u, j, :], tile_of(k.xres, t), column_of(k.rstd, t), column_of(k.nmr, t),
                                          ALU.mult, ALU.add).then_inc(f_xn_done, 1)
                    for j in range(2):
                        t = 2 * q + j
                        dve.wait_ge(f_xn_done, t + 1)
                        if later(q, 1):
                            dve.wait_ge(f_score_done, t - 1)
                        dve.tensor_tensor_reduce(junk[:, j, :], xn[:, u, j, :], k.w_r[:, :], 1.0, k.b_r[:, 0:1], ALU.mult, ALU.add,
                                                 score[:, u, j:j + 1]).then_inc(f_score_done, 1)
                if on[2]:
                    for j in range(2):
                        t = 2 * f + j
                        dve.wait_ge(f_returned, 2 * f + 2)
                        dve.tensor_tensor(tile_of(k.xres, t), b_back[:, j * D:(j + 1) * D], tile_of(k.xres, t),
                                          ALU.add).then_inc(f_x2, 1)
                if on[0]:
                    for j in range(2):
                        t = 2 * q + j
                        row, own = b_row[:, j * P:(j + 1) * P], score[:, u, j:j + 1]
                        dve.wait_ge(f_row, 2 * q + 2)
                        if later(q, 1):
                            dve.wait_ge(f_tied_done, t - 1)
                        dve.scalar_tensor_tensor(out=junk2[:, j, :], in0=row, scalar=own, in1=k.same[:, :], op0=ALU.is_gt,
                                                 op1=ALU.mult, accum_out=above[:, u, j:j + 1]).then_inc(f_above_done, 1)
                        dve.wait_ge(f_above_done, t + 1)
                        dve.scalar_tensor_tensor(out=junk2[:, j, :], in0=row, scalar=own, in1=k.earlier[:, :], op0=ALU.is_equal,
                                                 op1=ALU.mult, accum_out=tied[:, u, j:j + 1]).then_inc(f_tied_done, 1)
                    for j in range(2):
                        t = 2 * q + j
                        if later(q, 2):
                            dve.wait_ge(f_pickT, q - 1)
                        if on[2]:
                            dve.wait_ge(f_x2, 2 * f + j + 1)
                        dve.wait_ge(f_tied_done, t + 1)
                        dve.tensor_scalar(pick[:, u, j, j * 64:j * 64 + 64], k.slot[:, :], above[:, u, j:j + 1],
                                          tied[:, u, j:j + 1], ALU.subtract, ALU.is_equal).then_inc(f_pick_done, 1)
                if on[2]:
                    if not on[0]:
                        dve.wait_ge(f_x2, 2 * f + 2)
                    for j in range(2):
                        t = 2 * f + j
                        dve.bn_stats(tile_of(k.raw, t), tile_of(k.xres, t)).then_inc(f_raw, 1)
                if on[1]:
                    dve.wait_ge(f_y, m + 1)
                    if later(m, 2):
                        dve.wait_ge(f_returned, 2 * (m - 1))
                    dve.tensor_tensor(ys[:, v, :], b_y[:, 0:D], k.b2[:, :], ALU.add).then_inc(f_ys_done, 1)
            pipelined(dve, step, NQ, 3)
            dve.wait_ge(f_raw, NT)
        inner.close()
        z.end()


def second_attention(nc, ins, k, bank):
    with ExitStack() as stack:
        z = Scope(nc, stack)
        ctx_t = z.sb("g_ctx_t", [P, 2, P])
        ctx_k = z.sb("g_ctx_k", [P, 2, P])
        xn = z.sb("g_xn", [P, 2, D])
        xn_t = z.sb("g_xn_t", [P, 2, KC, P])
        qk = z.sb("g_qk", [P, 2, 2 * D])
        sq = z.sb("g_sq", [P, 2, 2 * D])
        cen = z.sb("g_cen", [P, 2, 2 * D])
        hat = z.sb("g_hat", [P, 2, 2 * D])
        sums = z.sb("g_sums", [P, 2, 2 * H1])
        tot, var = z.sb("g_tot", [P, 2, 2 * H1]), z.sb("g_var", [P, 2, 2 * H1])
        hlnv, hrstd = z.sb("g_hlnv", [P, 2, 2 * H1]), z.sb("g_hrstd", [P, 2, 2 * H1])
        q_t = z.sb("g_q_t", [P, 2, KC, P])
        k_t = z.sb("g_k_t", [P, 2, KC, P])
        k_bd = z.sb("g_k_bd", [P, 2, KC, 2, HG1, S])
        top = z.sb("g_top", [P, KC, 2, HG1])
        sub = z.sb("g_sub", [P, KC, BANK])
        pr_t = z.sb("g_pr_t", [P, KC, NHC1, P])
        v_bd = z.sb("g_v_bd", [P, 2, 2, NHP1, VW1])
        rcp = z.sb("g_rcp", [P, KC, NHC1, 4])
        halves = z.sb("g_halves", [P, 2, NHP1, 2, 2 * HD1])
        att = z.sb("g_att", [P, 2, D])
        att_t = z.sb("g_att_t", [P, 2, KC, P])
        vbias = z.sb("g_vbias", [P, D])
        head_eps = z.sb("g_head_eps", [P, 1])

        (g_ctx0, g_ctx1, g_fill, g_stats, g_rowln, g_rowrstd, g_rownmr, g_xn_s, g_xnT, g_xnTc, g_qkp, g_qk_s,
         g_sums_s, g_tot_s, g_cen_s, g_sq_s, g_var_s, g_hln, g_hrstd_s, g_hat_s, g_hatT, g_qt, g_kt, g_kbd,
         g_vm, g_vd, g_vc, g_s, g_top_s, g_sub_s, g_prT, g_exp, g_pv, g_rcp_s, g_half, g_add, g_att_s,
         g_attT, g_attTc, g_out, g_bias, g_x3, g_raw_s
         ) = z.sems(
             "g_ctx0 g_ctx1 g_fill g_stats g_rowln g_rowrstd g_rownmr g_xn_s g_xnT g_xnTc g_qkp g_qk_s g_sums_s "
             "g_tot_s g_cen_s g_sq_s g_var_s g_hln g_hrstd_s g_hat_s g_hatT g_qt g_kt g_kbd g_vm g_vd g_vc g_s "
             "g_top_s g_sub_s g_prT g_exp g_pv g_rcp_s g_half g_add g_att_s g_attT g_attTc g_out g_bias g_x3 "
             "g_raw_s")
        ctx_in = [g_ctx0, g_ctx1]
        b_turn, b_qk, b_hat, b_v, b_s, b_pr, b_o = bank[0], bank[1], bank[2], bank[3], bank[4:6], bank[6], bank[7]
        NM = 2 * MAIN

        inner = stack.enter_context(ExitStack())
        block = inner.enter_context(nc.Block())

        @block.sync
        def _(sp):
            def load(t, i, u):
                if later(t, 2):
                    sp.wait_ge(ctx_in[u], 32 * i)
                    sp.wait_ge(g_qkp, t - 1)
                    sp.wait_ge(g_vd, t - 1)
                sp.dma_start(ctx_t[:, u, :], ins["ctx_t"][:, bass.ds(t * P, P)]).then_inc(ctx_in[u], 16)
                sp.dma_start(ctx_k[:, u, :], ins["ctx_keys_t"][:, bass.ds(t * P, P)]).then_inc(ctx_in[u], 16)

            load(0, 0, 0)
            load(1, 0, 1)
            with sp.Fori(1, NT // 2) as i:
                for u in range(2):
                    load(2 * i + u, i, u)

        @block.gpsimd
        def _(pool):
            pool.memset(v_bd[:, :, :, :, :], 0.0).then_inc(g_fill, 1)
            pool.memset(head_eps[:, :], HEAD_EPS).then_inc(g_fill, 1)
            pool.wait_ge(k.loaded, 16 * len(k.later_loads))
            pool.tensor_tensor(vbias[:, :], k.bv1[:, :], k.bv1d[:, :], ALU.add).then_inc(g_fill, 1)
            pool.wait_ge(g_fill, 3)
            for h in range(2):
                rows = slice(64 * h, 64 * h + 64)
                for kind in range(2):
                    w = 2 * 2 * HD1 + 2 * kind + h
                    for ub in range(4):
                        pool.tensor_scalar(v_bd[rows, ub // 2, ub % 2, :, w:w + 1], v_bd[rows, ub // 2, ub % 2, :, w:w + 1],
                                           k.kind[rows, kind:kind + 1], None, ALU.add).then_inc(g_fill, 1)
                pool.wait_ge(g_fill, 3 + 8 * (h + 1))

            def step(n, i, u, on):
                t, tk, a, f = n, n - 1, n - 2, n - 3
                v = 1 - u
                if on[0]:
                    pool.wait_ge(g_xn_s, t + 1)
                    pool.tensor_tensor(tile_of(k.xres, t), tile_of(k.xres, t), k.bo1[:, :], ALU.add).then_inc(g_bias, 1)
                if on[1]:
                    pool.wait_ge(g_kt, 2 * tk + 2)
                    if later(tk, 2):
                        pool.wait_ge(g_s, KC * (tk - 1))
                    for c in range(KC):
                        for first, count, at in ((0, MAIN, 0), (NM, DCA, MAIN)):
                            for b in range(2):
                                pool.tensor_tensor(k_bd[:, v, c, b, :, at:at + count],
                                                   spread(k_t[:, v, c, first + b * count:first + (b + 1) * count], HG1),
                                                   stretch(k.head_mask1[:, :], count), ALU.mult).then_inc(g_kbd, 1)
                if on[0]:
                    pool.wait_ge(g_tot_s, t + 1)
                    if later(t, 2):
                        pool.wait_ge(g_hat_s, t - 1)
                    pool.tensor_tensor(cen[:, u, :].rearrange("p (h d) -> p h d", d=HD1), qk[:, u, :].rearrange("p (h d) -> p h d", d=HD1),
                                       stretch(tot[:, u, :], HD1), ALU.add).then_inc(g_cen_s, 1)
                if on[2]:
                    pool.wait_ge(g_half, KC * a + KC)
                    if later(a, 2):
                        pool.wait_ge(g_attT, a - 1)
                    pool.tensor_tensor(att[:, u, :].rearrange("p (n w) -> p n w", n=NHP1), halves[:, u, :, 0, :],
                                       halves[:, u, :, 1, :], ALU.add).then_inc(g_add, 1)
                    pool.wait_ge(g_add, a + 1)
                    pool.tensor_tensor(att[:, u, :], att[:, u, :], vbias[:, :], ALU.add).then_inc(g_att_s, 1)
            pipelined(pool, step, NT, 4)

        @block.tensor
        def _(pe):
            pe.wait_ge(k.loaded, 16 * len(k.later_loads))

            def scores(t, u, c):
                pe.wait_ge(g_kbd, 4 * KC * t + 4 * c + 4)
                if later(t, 1):
                    pe.wait_ge(g_sub_s, 2 * (KC * (t - 1) + c + 1))
                for b in range(2):
                    m = pe.matmul(b_s[c][64 * b:64 * b + 64, :], q_t[:, u, c, b * S:(b + 1) * S],
                                  k_bd[:, u, c, b, :, :].rearrange("p h k -> p (h k)"), start=True, stop=True)
                m.then_inc(g_s, 1)

            def turn(t, c):
                pe.wait_ge(g_sub_s, 2 * (KC * t + c + 1))
                if later(t, 1) or c >= 1:
                    pe.wait_ge(g_exp, KC * t + c)
                for j in range(NHC1):
                    m = pe.transpose(b_pr[:, j * P:(j + 1) * P], sub[:, c, j * P:(j + 1) * P], k.ident[:, :])
                m.then_inc(g_prT, 1)

            def values(t, u, c):
                pe.wait_ge(g_exp, KC * t + c + 1)
                if c == 0:
                    pe.wait_ge(g_vc, 4 * t + 4)
                if later(t, 1) or c >= 1:
                    pe.wait_ge(g_half, KC * t + c)
                for j in range(NHC1):
                    for b in range(2):
                        m = pe.matmul(b_o[64 * b:64 * b + 64, j * VW1:(j + 1) * VW1], pr_t[:, c, j, b * S:(b + 1) * S],
                                      v_bd[:, u, b, NHC1 * c + j, :], start=True, stop=True)
                m.then_inc(g_pv, 1)

            def value_rows(w, u, done):
                for b in range(2):
                    for h in range(2):
                        m = pe.matmul(b_v[64 * h:64 * h + 64, b * D:(b + 1) * D], ctx_t[:, u, b * S:(b + 1) * S],
                                      w, start=True, stop=True)
                m.then_inc(done, 1)

            def step(n, i, u, on):
                t, tk, a, f = n, n - 1, n - 2, n - 3
                v = 1 - u
                if on[2]:
                    scores(a, u, 0)
                    scores(a, u, 1)
                if on[3]:
                    pe.wait_ge(g_att_s, f + 1)
                    if later(f, 1):
                        pe.wait_ge(g_x3, f)
                    pe.wait_ge(g_xnTc, n if on[0] else NT)
                    for c in range(KC):
                        m = pe.transpose(b_turn[:, c * P:(c + 1) * P], att[:, v, c * P:(c + 1) * P], k.ident[:, :])
                    m.then_inc(g_attT, 1)
                if on[1]:
                    pe.wait_ge(g_hat_s, tk + 1)
                    if later(tk, 1):
                        pe.wait_ge(g_qt, tk)
                        pe.wait_ge(g_kt, 2 * tk)
                    for c in range(2 * KC):
                        m = pe.transpose(b_hat[:, c * P:(c + 1) * P], hat[:, v, c * P:(c + 1) * P], k.ident[:, :])
                    m.then_inc(g_hatT, 1)
                    if later(tk, 1):
                        pe.wait_ge(g_vc, 4 * tk)
                    value_rows(k.wv1[:, :], v, g_vm)
                if on[2]:
                    turn(a, 0)
                if on[3]:
                    pe.wait_ge(g_attTc, f + 1)
                    for c in range(KC):
                        m = pe.matmul(b_turn[:, D:2 * D], att_t[:, v, c, :], k.wo1[:, c, :], start=(c == 0), stop=(c == KC - 1))
                    m.then_inc(g_out, 1)
                if on[2]:
                    turn(a, 1)
                    values(a, u, 0)
                if on[0]:
                    pe.wait_ge(g_xn_s, t + 1)
                    if on[3]:
                        pe.wait_ge(g_x3, f + 1)
                    for c in range(KC):
                        m = pe.transpose(b_turn[:, c * P:(c + 1) * P], xn[:, u, c * P:(c + 1) * P], k.ident[:, :])
                    m.then_inc(g_xnT, 1)
                if on[1]:
                    pe.wait_ge(g_vc, 4 * tk + 2)
                    value_rows(k.wkv1d[:, D:2 * D], v, g_vd)
                if on[2]:
                    values(a, u, 1)
                if on[0]:
                    pe.wait_ge(ctx_in[u], 32 * (i + 1))
                    pe.wait_ge(g_xnTc, t + 1)
                    if later(t, 1):
                        pe.wait_ge(g_qk_s, t)
                    for c in range(KC):
                        pe.matmul(b_qk[:, 0:D], xn_t[:, u, c, :], k.wq1[:, c, :], start=(c == 0), stop=(c == KC - 1))
                    pe.matmul(b_qk[0:NM, D:2 * D], ctx_k[:, u, 0:NM], k.wk1[:, :], start=True, stop=True)
                    pe.matmul(b_qk[NM:P, D:2 * D], ctx_k[:, u, NM:P], k.wkv1d[:, 0:D], start=True, stop=True).then_inc(g_qkp, 1)
            pipelined(pe, step, NT, 4)

        @block.scalar
        def _(act):
            act.preload_act_table_set("natural_log_exp_and_others")
            row_scales(act, k, g_stats, g_rowln, g_rowrstd)
            act.wait_ge(g_fill, 3 + 16)
            act.wait_ge(k.loaded, 16 * len(k.later_loads))

            def step(n, i, u, on):
                t, tk, a, f = n, n - 1, n - 2, n - 3
                v = 1 - u

                def exps(c):
                    act.wait_ge(g_prT, KC * a + c + 1)
                    if later(a, 1):
                        act.wait_ge(g_pv, KC * (a - 1) + c + 1)
                    act.activation(pr_t[:, c, :, :].rearrange("p j q -> p (j q)"), b_pr[:, :], ACT.Exp).then_inc(g_exp, 1)

                def keep_values(kind, done):
                    act.wait_ge(done, tk + 1)
                    vp = b_v[:, :].rearrange("p (b n h d) -> p b n h d", b=2, n=NHP1, h=2)
                    for h in range(2):
                        rows = slice(64 * h, 64 * h + 64)
                        o = (2 * kind + h) * HD1
                        act.activation(v_bd[rows, v, :, :, o:o + HD1], vp[rows, :, :, h, :], ACT.Copy,
                                       scale=k.kind[rows, kind:kind + 1]).then_inc(g_vc, 1)

                if on[3]:
                    act.wait_ge(g_attT, f + 1)
                    act.activation(att_t[:, v, :, :].rearrange("p c q -> p (c q)"), b_turn[:, 0:D], ACT.Copy).then_inc(g_attTc, 1)
                if on[1]:
                    act.wait_ge(g_hatT, tk + 1)
                    if later(tk, 2):
                        act.wait_ge(g_s, KC * (tk - 1))
                        act.wait_ge(g_kbd, 4 * KC * (tk - 1))
                    act.activation(q_t[:, v, :, :].rearrange("p c q -> p (c q)"), b_hat[:, 0:D], ACT.Identity,
                                   scale=k.norms[:, 0:1], bias=k.norms[:, 1:2]).then_inc(g_qt, 1)
                    kp = b_hat[:, D:2 * D].rearrange("p (c s) -> p c s", c=KC)
                    for cols, w in ((slice(0, NM), 2), (slice(NM, P), 4)):
                        act.activation(k_t[:, v, :, cols], kp[:, :, cols], ACT.Identity,
                                       scale=k.norms[:, w:w + 1], bias=k.norms[:, w + 1:w + 2]).then_inc(g_kt, 1)
                    if later(tk, 2):
                        act.wait_ge(g_pv, KC * (tk - 1))
                    keep_values(0, g_vm)
                if on[2]:
                    exps(0)
                    exps(1)
                if on[0]:
                    act.wait_ge(g_xnT, t + 1)
                    act.activation(xn_t[:, u, :, :].rearrange("p c q -> p (c q)"), b_turn[:, 0:D], ACT.Copy).then_inc(g_xnTc, 1)
                if on[1]:
                    keep_values(1, g_vd)
                if on[0]:
                    act.wait_ge(g_cen_s, t + 1)
                    if later(t, 2):
                        act.wait_ge(g_var_s, t - 1)
                    act.activation(sq[:, u, :], cen[:, u, :], ACT.Square).then_inc(g_sq_s, 1)
                    act.wait_ge(g_var_s, t + 1)
                    act.activation(hlnv[:, u, :], var[:, u, :], ACT.Ln, scale=1.0 / HD1, bias=head_eps[:, 0:1]).then_inc(g_hln, 1)
                    act.wait_ge(g_hln, t + 1)
                    act.activation(hrstd[:, u, :], hlnv[:, u, :], ACT.Exp, scale=-0.5).then_inc(g_hrstd_s, 1)
            pipelined(act, step, NT, 4)

        @block.vector
        def _(dve):
            row_statistics(dve, k, g_stats)
            row_shifts(dve, k, g_rowrstd, g_rownmr)
            dve.wait_ge(k.loaded, 16 * len(k.later_loads))

            def step(n, i, u, on):
                t, a, f = n, n - 2, n - 3
                v = 1 - u

                def softmax_part(c):
                    sc = b_s[c][:, :].rearrange("p (h k) -> p h k", k=S)
                    su = sub[:, c, :].rearrange("p (h k) -> p h k", k=S)
                    parts = ((0, slice(0, MAIN), MAIN), (1, slice(MAIN, S), DCA))
                    dve.wait_ge(g_s, KC * a + c + 1)
                    for kind, keys, _ in parts:
                        dve.tensor_reduce(top[:, c, kind, :], sc[:, :, keys], AX.X, ALU.max).then_inc(g_top_s, 1)
                    if later(a, 1):
                        dve.wait_ge(g_prT, KC * (a - 1) + c + 1)
                    for kind, keys, count in parts:
                        dve.wait_ge(g_top_s, 2 * (KC * a + c) + kind + 1)
                        dve.tensor_tensor(su[:, :, keys], sc[:, :, keys], stretch(top[:, c, kind, :], count),
                                          ALU.subtract).then_inc(g_sub_s, 1)

                def divide(c):
                    o3 = b_o[:, 0:NHC1 * VW1].rearrange("p (n w) -> p n w", w=VW1)
                    dve.wait_ge(g_pv, KC * a + c + 1)
                    dve.reciprocal(rcp[:, c, :, :], o3[:, :, 2 * 2 * HD1:VW1]).then_inc(g_rcp_s, 1)
                    dve.wait_ge(g_rcp_s, KC * a + c + 1)
                    if c == 0 and later(a, 2):
                        dve.wait_ge(g_add, a - 1)
                    dve.tensor_tensor(halves[:, u, NHC1 * c:NHC1 * (c + 1), :, :].rearrange("p n e (h d) -> p n (e h) d", h=2),
                                      o3[:, :, 0:2 * 2 * HD1].rearrange("p n (w d) -> p n w d", d=HD1),
                                      rcp[:, c, :, :].rearrange("p n (w a) -> p n w a", a=1).to_broadcast([P, NHC1, 4, HD1]),
                                      ALU.mult).then_inc(g_half, 1)

                if on[0]:
                    if later(t, 2):
                        dve.wait_ge(g_xnT, t - 1)
                    dve.tensor_scalar(xn[:, u, :], tile_of(k.xres, t), column_of(k.rstd, t), column_of(k.nmr, t),
                                      ALU.mult, ALU.add).then_inc(g_xn_s, 1)
                if on[2]:
                    softmax_part(0)
                    softmax_part(1)
                if on[3]:
                    dve.wait_ge(g_out, f + 1)
                    dve.wait_ge(g_bias, f + 1)
                    dve.tensor_tensor(tile_of(k.xres, f), b_turn[:, D:2 * D], tile_of(k.xres, f), ALU.add).then_inc(g_x3, 1)
                    dve.wait_ge(g_x3, f + 1)
                if on[2]:
                    divide(0)
                if on[3]:
                    dve.bn_stats(tile_of(k.raw, f), tile_of(k.xres, f)).then_inc(g_raw_s, 1)
                if on[0]:
                    dve.wait_ge(g_qkp, t + 1)
                    if later(t, 2):
                        dve.wait_ge(g_cen_s, t - 1)
                    dve.tensor_tensor(qk[:, u, :], b_qk[:, :], k.bqk1[:, :], ALU.add).then_inc(g_qk_s, 1)
                    dve.wait_ge(g_qk_s, t + 1)
                    dve.tensor_reduce(sums[:, u, :], qk[:, u, :].rearrange("p (h d) -> p h d", d=HD1), AX.X, ALU.add).then_inc(g_sums_s, 1)
                    dve.wait_ge(g_sums_s, t + 1)
                    if later(t, 2):
                        dve.wait_ge(g_cen_s, t - 1)
                    dve.tensor_scalar(tot[:, u, :], sums[:, u, :], -1.0 / HD1, None, ALU.mult).then_inc(g_tot_s, 1)
                if on[2]:
                    divide(1)
                if on[0]:
                    dve.wait_ge(g_sq_s, t + 1)
                    dve.tensor_reduce(var[:, u, :], sq[:, u, :].rearrange("p (h d) -> p h d", d=HD1), AX.X, ALU.add).then_inc(g_var_s, 1)
                    dve.wait_ge(g_hrstd_s, t + 1)
                    if later(t, 2):
                        dve.wait_ge(g_hatT, t - 1)
                    dve.tensor_tensor(hat[:, u, :].rearrange("p (h d) -> p h d", d=HD1), cen[:, u, :].rearrange("p (h d) -> p h d", d=HD1),
                                      stretch(hrstd[:, u, :], HD1), ALU.mult).then_inc(g_hat_s, 1)
            pipelined(dve, step, NT, 4)
            dve.wait_ge(g_raw_s, NT)
        inner.close()
        z.end()


def route(nc, ins, k, bank, out, table):
    with ExitStack() as stack:
        z = Scope(nc, stack)
        row = z.sb("r_row", [P, 2, ROW])
        xn_t = z.sb("r_xn_t", [P, 2, KC, P])
        best = z.sb("r_best", [P, 2, TOPK])
        neg = z.sb("r_neg", [P, 2])
        marked = z.sb("r_marked", [P, 2, E])
        ex = z.sb("r_ex", [P, 2, E])
        chosen = z.sb("r_chosen", [P, 2, E])
        total, share = z.sb("r_total", [P, 2]), z.sb("r_share", [P, 2])
        vals = z.sb("r_vals", [P, 2 * E])
        zero = z.sb("r_zero", [P, ROW])
        (r_fill, r_stats, r_rowln, r_rowrstd, r_rownmr, r_xn, r_xnT, r_xnTc, r_log, r_best_s, r_neg_s,
         r_marked_s, r_ex_s, r_chosen_s, r_share_s, r_w, r_vals_s, r_valsT, r_found, r_row0, r_row1, r_x3,
         r_pad
         ) = z.sems(
             "r_fill r_stats r_rowln r_rowrstd r_rownmr r_xn r_xnT r_xnTc r_log r_best_s r_neg_s r_marked_s r_ex_s "
             "r_chosen_s r_share_s r_w r_vals_s r_valsT r_found r_row0 r_row1 r_x3 r_pad")
        row_out = [r_row0, r_row1]
        b_turn, b_log, b_vals = bank[0], bank[1:3], bank[3]

        def tile_at(i, u, stage):
            if stage == 1:
                return i if u else i - 1 + NT // 2
            return i - stage // 2 + u * (NT // 2)

        inner = stack.enter_context(ExitStack())
        block = inner.enter_context(nc.Block())

        @block.sync
        def _(sp):
            sp.dma_start(out[0:T, :].rearrange("(t p) d -> p t d", p=P), k.xres[:, :, :]).then_inc(r_x3, 16)
            sp.wait_ge(r_fill, 1)
            sp.dma_start(out[T:T + P, :], zero[:, 0:D]).then_inc(r_pad, 16)
            sp.dma_start(table[T:T + P, :], zero[:, :]).then_inc(r_pad, 16)

            def step(n, i, u, on):
                if on[1]:
                    m, v, t = n - 1, 1 - u, tile_at(i, u, 1)
                    sp.wait_ge(r_w, m + 1)
                    sp.dma_start(table[bass.ds(t * P, P), :], row[:, v, :]).then_inc(row_out[v], 16)
            pipelined(sp, step, NT, 2)
            for v in range(2):
                sp.wait_ge(row_out[v], 16 * (NT // 2))
            sp.wait_ge(r_pad, 32)
            sp.wait_ge(r_x3, 16)

        @block.gpsimd
        def _(pool):
            pool.memset(zero[:, :], 0.0).then_inc(r_fill, 1)

        @block.tensor
        def _(pe):
            def step(n, i, u, on):
                if on[2] and u == 1:
                    pe.wait_ge(r_vals_s, n - 1)
                    if later(n - 2, 2):
                        pe.wait_ge(r_found, i - 1)
                    pe.transpose(b_vals[:, 0:P], vals[:, :], k.ident[:, :]).then_inc(r_valsT, 1)
                if on[0]:
                    pe.wait_ge(r_xn, n + 1)
                    if later(n, 1):
                        pe.wait_ge(r_xnTc, n)
                    for c in range(KC):
                        m = pe.transpose(b_turn[:, c * P:(c + 1) * P], row[:, u, c * P:(c + 1) * P], k.ident[:, :])
                    m.then_inc(r_xnT, 1)
                    pe.wait_ge(r_xnTc, n + 1)
                    if later(n, 2):
                        pe.wait_ge(r_marked_s, n - 1)
                        pe.wait_ge(r_ex_s, n - 1)
                    for c in range(KC):
                        m = pe.matmul(b_log[u][:, 0:E], xn_t[:, u, c, :], k.gate[:, c, :], start=(c == 0), stop=(c == KC - 1))
                    m.then_inc(r_log, 1)
            pipelined(pe, step, NT, 3)

        @block.scalar
        def _(act):
            row_scales(act, k, r_stats, r_rowln, r_rowrstd)

            def step(n, i, u, on):
                if on[1]:
                    m, v = n - 1, 1 - u
                    act.wait_ge(r_neg_s, m + 1)
                    act.wait_ge(r_marked_s, m + 1)
                    if later(m, 2):
                        act.wait_ge(r_chosen_s, m - 1)
                    act.activation(ex[:, v, :], b_log[v][:, 0:E], ACT.Exp, bias=neg[:, v:v + 1]).then_inc(r_ex_s, 1)
                if on[2] and u == 1:
                    act.wait_ge(r_valsT, i)
                    act.activation(k.found[:, bass.ds((i - 1) * P, P)], b_vals[:, 0:P], ACT.Copy).then_inc(r_found, 1)
                if on[0]:
                    act.wait_ge(r_xnT, n + 1)
                    if later(n, 2):
                        act.wait_ge(r_log, n - 1)
                    act.activation(xn_t[:, u, :, :].rearrange("p c q -> p (c q)"), b_turn[:, 0:D], ACT.Copy).then_inc(r_xnTc, 1)
            pipelined(act, step, NT, 3)

        @block.vector
        def _(dve):
            row_statistics(dve, k, r_stats)
            row_shifts(dve, k, r_rowrstd, r_rownmr)

            def step(n, i, u, on):
                if on[1]:
                    dve.wait_ge(r_log, n)
                if on[0]:
                    t = tile_at(i, u, 0)
                    if later(n, 2):
                        dve.wait_ge(row_out[u], 16 * i)
                        dve.wait_ge(r_xnT, n - 1)
                    dve.tensor_scalar(row[:, u, 0:D], tile_of(k.xres, t), column_of(k.rstd, t), column_of(k.nmr, t),
                                      ALU.mult, ALU.add).then_inc(r_xn, 1)
                if on[1]:
                    m, v, t = n - 1, 1 - u, tile_at(i, u, 1)
                    dve.max(best[:, v, :], b_log[v][:, 0:E]).then_inc(r_best_s, 1)
                    dve.wait_ge(r_best_s, m + 1)
                    if later(m, 2):
                        dve.wait_ge(r_ex_s, m - 1)
                    dve.tensor_scalar(neg[:, v:v + 1], best[:, v, 0:1], -1.0, None, ALU.mult).then_inc(r_neg_s, 1)
                    dve.match_replace(marked[:, v, :], best[:, v, :], b_log[v][:, 0:E], TAKEN).then_inc(r_marked_s, 1)
                    dve.wait_ge(r_marked_s, m + 1)
                    if v == 0 and later(m, 2):
                        dve.wait_ge(r_valsT, i)
                    dve.tensor_scalar(vals[:, E * v:E * v + E], marked[:, v, :], TAKEN, column_of(k.countdown, t),
                                      ALU.is_equal, ALU.mult).then_inc(r_vals_s, 1)
                    dve.wait_ge(r_ex_s, m + 1)
                    dve.scalar_tensor_tensor(out=chosen[:, v, :], in0=marked[:, v, :], scalar=TAKEN, in1=ex[:, v, :],
                                             op0=ALU.is_equal, op1=ALU.mult, accum_out=total[:, v:v + 1]).then_inc(r_chosen_s, 1)
                    dve.wait_ge(r_chosen_s, m + 1)
                    dve.reciprocal(share[:, v:v + 1], total[:, v:v + 1]).then_inc(r_share_s, 1)
                    dve.wait_ge(r_share_s, m + 1)
                    dve.tensor_scalar(row[:, v, D:ROW], chosen[:, v, :], share[:, v:v + 1], None, ALU.mult).then_inc(r_w, 1)
            pipelined(dve, step, NT, 3)
        inner.close()
        z.end()


def fill_slots(nc, ins, k, bank):
    with ExitStack() as stack:
        z = Scope(nc, stack)
        best = z.sb("s_best", [P, CAP])
        best_t = z.sb("s_best_t", [CAP, P])
        both = z.sb("s_both", [E, P])
        first = z.sb("s_first", [E, 2, CAP])
        value = z.sb("s_value", [P, NP_E])
        empty, name = z.sb("s_empty", [P, NP_E]), z.sb("s_name", [P, NP_E])
        (s_max, s_rep, s_turn, s_turnc, s_back, s_backc, s_max2, s_rep2, s_dup, s_last, s_value_s, s_empty_s,
         s_name_s, s_token, s_move
         ) = z.sems(
             "s_max s_rep s_turn s_turnc s_back s_backc s_max2 s_rep2 s_dup s_last s_value_s s_empty_s s_name_s "
             "s_token s_move")
        rounds = CAP // 8
        inner = stack.enter_context(ExitStack())
        block = inner.enter_context(nc.Block())

        def first_of(dve, found, best, max_done, rep_done):
            for r in range(rounds):
                if r:
                    dve.wait_ge(rep_done, r)
                dve.max(best[:, 8 * r:8 * r + 8], found).then_inc(max_done, 1)
                if r < rounds - 1:
                    dve.wait_ge(max_done, r + 1)
                    dve.match_replace(found, best[:, 8 * r:8 * r + 8], found, 0.0).then_inc(rep_done, 1)

        @block.vector
        def _(dve):
            first_of(dve, k.found[:, :], best, s_max, s_rep)
            dve.wait_ge(s_backc, 1)
            first_of(dve, both[:, :], first[:, 0, :], s_max2, s_rep2)
            dve.wait_ge(s_max2, rounds)
            dve.tensor_copy(first[:, 1, :], first[:, 0, :]).then_inc(s_dup, 1)
            dve.wait_ge(s_last, 1)
            for h in range(2):
                rows = slice(64 * h, 64 * h + 64)
                dve.tensor_copy(value[rows, :], bank[2][rows, 0:E].rearrange("p (j e) -> p j e", e=2)[:, :, h]).then_inc(s_value_s, 1)
            dve.wait_ge(s_value_s, 2)
            dve.tensor_scalar(empty[:, :], value[:, :], 0.0, k.row_number[:, 0:1], ALU.is_equal, ALU.mult).then_inc(s_empty_s, 1)
            dve.tensor_scalar(name[:, :], value[:, :], -1.0, float(T), ALU.mult, ALU.add).then_inc(s_name_s, 1)
            dve.wait_ge(s_empty_s, 1)
            dve.wait_ge(s_name_s, 1)
            dve.tensor_tensor(k.token[:, :], empty[:, :], name[:, :], ALU.add).then_inc(s_token, 1)
            dve.wait_ge(s_token, 1)
            dve.tensor_scalar(k.move[:, :], k.token[:, :], -1.0, k.spare_row[:, 0:1], ALU.mult, ALU.add).then_inc(s_move, 1)
            dve.wait_ge(s_move, 1)

        @block.tensor
        def _(pe):
            pe.wait_ge(s_max, rounds)
            pe.transpose(bank[0][0:CAP, 0:P], best[:, :], k.ident[:, :]).then_inc(s_turn, 1)
            pe.wait_ge(s_turnc, 1)
            for h in range(2):
                m = pe.transpose(bank[1][0:E, h * CAP:(h + 1) * CAP], best_t[:, h * E:(h + 1) * E], k.ident[0:CAP, 0:CAP])
            m.then_inc(s_back, 1)
            pe.wait_ge(s_dup, 1)
            pe.transpose(bank[2][:, 0:E], first[:, :, :].rearrange("e a c -> e (a c)"), k.ident[0:E, 0:E]).then_inc(s_last, 1)

        @block.scalar
        def _(act):
            act.wait_ge(s_turn, 1)
            act.activation(best_t[:, :], bank[0][0:CAP, 0:P], ACT.Copy).then_inc(s_turnc, 1)
            act.wait_ge(s_back, 1)
            act.activation(both[:, :], bank[1][0:E, 0:P], ACT.Copy).then_inc(s_backc, 1)
        inner.close()
        z.end()


def experts(nc, ins, k, bank, out, table):
    with ExitStack() as stack:
        z = Scope(nc, stack)
        w_g, w_u = z.sb("e_w_g", [P, 2, 2, KC, I]), z.sb("e_w_u", [P, 2, 2, KC, I])
        w_d = z.sb("e_w_d", [I, 2, 2, D])
        tok = z.sb("e_tok", [P, 2])
        idx = z.sb("e_idx", [P, 2], U32)
        to = z.sb("e_to", [P, 2], U32)
        got = z.sb("e_got", [P, 2, ROW])
        got_t = z.sb("e_got_t", [P, 2, KC, P])
        twin = z.sb("e_twin", [P, 2, P])
        count, again = z.sb("e_count", [P, 2]), z.sb("e_again", [P, 2])
        wcol = z.sb("e_wcol", [P, 2])
        act_g = z.sb("e_act_g", [I, 2, P])
        hid = z.sb("e_hid", [I, 2, P])
        part = z.sb("e_part", [P, 2, D])
        add = z.sb("e_add", [P, 2, D])
        pace = z.sb("e_pace", [P, 3])
        (e_w0, e_w1, e_tok_s, e_idx_s, e_got0, e_got1, e_row, e_twin_s, e_again_s, e_to_s, e_gotT, e_gotTc,
         e_gu, e_silu, e_hid_s, e_y, e_wcol_s, e_part_s, e_sum, e_add_s, e_added, e_pace_fill, e_pace_get,
         e_pace_add
         ) = z.sems(
             "e_w0 e_w1 e_tok_s e_idx_s e_got0 e_got1 e_row e_twin_s e_again_s e_to_s e_gotT e_gotTc e_gu e_silu "
             "e_hid_s e_y e_wcol_s e_part_s e_sum e_add_s e_added e_pace_fill e_pace_get e_pace_add")
        w_in, got_in = [e_w0, e_w1], [e_got0, e_got1]
        b_row, b_turn, b_gu, b_y, b_sum = bank[0], bank[1], bank[2:4], bank[4], bank[5]
        inner = stack.enter_context(ExitStack())
        block = inner.enter_context(nc.Block())

        @block.sync
        def _(sp):
            def load(j, i, u):
                if later(j, 2):
                    sp.wait_ge(w_in[u], 48 * i)
                    sp.wait_ge(e_y, j - 1)
                for dst, name in ((w_g, "L1_ffn_wg"), (w_u, "L1_ffn_wu")):
                    sp.dma_start(dst[:, u, :, :, :].rearrange("p e c i -> p (e c) i"),
                                 ins[name].rearrange("e (c p) i -> p (e c) i", p=P)[:, bass.ds(2 * KC * j, 2 * KC), :]
                                 ).then_inc(w_in[u], 16)
                sp.dma_start(w_d[:, u, :, :], ins["L1_ffn_wd"].rearrange("e i d -> i e d")[:, bass.ds(2 * j, 2), :]).then_inc(w_in[u], 16)
            load(0, 0, 0)
            load(1, 0, 1)
            with sp.Fori(1, NP_E // 2) as i:
                for u in range(2):
                    load(2 * i + u, i, u)

        @block.gpsimd
        def _(pool):
            pool.memset(pace[:, :], 0.0).then_inc(e_pace_fill, 1)
            pool.wait_ge(e_pace_fill, 1)

            def step(n, i, u, on):
                if on[0]:
                    if later(n, 1):
                        pool.wait_ge(e_pace_get, n)
                    if later(n, 2):
                        pool.wait_ge(e_gotT, n - 1)
                        pool.wait_ge(e_wcol_s, 2 * (n - 1))
                    pool.wait_ge(e_idx_s, n + 1)
                    pool.tensor_tensor(pace[:, 0:1], pace[:, 2:3], pace[:, 2:3], ALU.add).then_inc(e_pace_get, 1)
                    pool.indirect_dma_start(out=got[:, u, :], out_offset=None, in_=table[:, :],
                                            in_offset=bass.IndirectOffsetOnAxis(ap=idx[:, u:u + 1], axis=0)).then_inc(got_in[u], 16)
                if on[2]:
                    j = n - 2
                    if later(j, 1):
                        pool.wait_ge(e_pace_add, j)
                        pool.wait_ge(e_added, 16 * j)
                    pool.wait_ge(e_add_s, j + 1)
                    pool.tensor_tensor(pace[:, 1:2], pace[:, 2:3], pace[:, 2:3], ALU.add).then_inc(e_pace_add, 1)
                    pool.indirect_dma_start(out=out[:, :], out_offset=bass.IndirectOffsetOnAxis(ap=to[:, u:u + 1], axis=0),
                                            in_=add[:, u, :], in_offset=None, compute_op=ALU.add).then_inc(e_added, 16)
            pipelined(pool, step, NP_E, 3)
            pool.wait_ge(e_added, 16 * NP_E)

        @block.tensor
        def _(pe):
            def step(n, i, u, on):
                v = 1 - u
                if on[2]:
                    j = n - 2
                    pe.wait_ge(e_part_s, j + 1)
                    if later(j, 1):
                        pe.wait_ge(e_add_s, j)
                    pe.matmul(b_sum[:, 0:D], twin[:, u, :], part[:, u, :], start=True, stop=True).then_inc(e_sum, 1)
                if on[0]:
                    pe.wait_ge(e_tok_s, n + 1)
                    if later(n, 1):
                        pe.wait_ge(e_twin_s, n)
                    pe.transpose(b_row[:, 0:P], tok[:, u:u + 1].to_broadcast([P, P]), k.ident[:, :]).then_inc(e_row, 1)
                if on[1]:
                    j = n - 1
                    pe.wait_ge(got_in[v], 16 * (i + u))
                    if later(j, 1):
                        pe.wait_ge(e_gotTc, j)
                    for c in range(KC):
                        m = pe.transpose(b_turn[:, c * P:(c + 1) * P], got[:, v, c * P:(c + 1) * P], k.ident[:, :])
                    m.then_inc(e_gotT, 1)
                    pe.wait_ge(e_gotTc, j + 1)
                    pe.wait_ge(w_in[v], 48 * (i + u))
                    if later(j, 2):
                        pe.wait_ge(e_hid_s, j - 1)
                    for w, o in ((w_g, 0), (w_u, P)):
                        for e in range(2):
                            for c in range(KC):
                                m = pe.matmul(b_gu[v][0:I, o + e * CAP:o + (e + 1) * CAP], w[:, v, e, c, :],
                                              got_t[:, v, c, e * CAP:(e + 1) * CAP], start=(c == 0), stop=(c == KC - 1))
                    m.then_inc(e_gu, 1)
                    pe.wait_ge(e_hid_s, j + 1)
                    if later(j, 1):
                        pe.wait_ge(e_part_s, j)
                    for e in range(2):
                        m = pe.matmul(b_y[e * CAP:(e + 1) * CAP, 0:D], hid[:, v, e * CAP:(e + 1) * CAP], w_d[:, v, e, :],
                                      start=True, stop=True)
                    m.then_inc(e_y, 1)
            pipelined(pe, step, NP_E, 3)

        @block.scalar
        def _(act):
            act.preload_act_table(ACT.Silu)

            def step(n, i, u, on):
                v = 1 - u
                if on[2]:
                    j = n - 2
                    act.wait_ge(e_sum, j + 1)
                    if later(j, 2):
                        act.wait_ge(e_added, 16 * (j - 1))
                    act.activation(add[:, u, :], b_sum[:, 0:D], ACT.Copy).then_inc(e_add_s, 1)
                if on[1]:
                    j = n - 1
                    act.wait_ge(e_gotT, j + 1)
                    if later(j, 2):
                        act.wait_ge(e_gu, j - 1)
                    act.activation(got_t[:, v, :, :].rearrange("p c q -> p (c q)"), b_turn[:, 0:D], ACT.Copy).then_inc(e_gotTc, 1)
                    act.wait_ge(e_gu, j + 1)
                    if later(j, 2):
                        act.wait_ge(e_hid_s, j - 1)
                    act.activation(act_g[:, v, :], b_gu[v][0:I, 0:P], ACT.Silu).then_inc(e_silu, 1)
            pipelined(act, step, NP_E, 3)

        @block.vector
        def _(dve):
            def step(n, i, u, on):
                v = 1 - u
                if on[0]:
                    if later(n, 2):
                        dve.wait_ge(e_to_s, n - 1)
                        dve.wait_ge(got_in[u], 16 * i)
                        dve.wait_ge(e_row, n - 1)
                    dve.tensor_copy(tok[:, u:u + 1], column_of(k.token, n)).then_inc(e_tok_s, 1)
                    dve.tensor_copy(idx[:, u:u + 1], column_of(k.token, n)).then_inc(e_idx_s, 1)
                if on[1]:
                    j = n - 1
                    dve.wait_ge(got_in[v], 16 * (i + u))
                    if later(j, 2):
                        dve.wait_ge(e_part_s, j - 1)
                    for h in range(2):
                        rows = slice(64 * h, 64 * h + 64)
                        dve.tensor_copy(wcol[rows, v:v + 1], got[rows, v, bass.ds(D + 2 * j + h, 1)]).then_inc(e_wcol_s, 1)
                    dve.wait_ge(e_silu, j + 1)
                    if later(j, 2):
                        dve.wait_ge(e_y, j - 1)
                    dve.tensor_tensor(hid[:, v, :], act_g[:, v, :], b_gu[v][0:I, P:2 * P], ALU.mult).then_inc(e_hid_s, 1)
                if on[0]:
                    dve.wait_ge(e_row, n + 1)
                    dve.wait_ge(e_tok_s, n + 1)
                    if later(n, 2):
                        dve.wait_ge(e_sum, n - 1)
                    dve.tensor_scalar(twin[:, u, :], b_row[:, 0:P], tok[:, u:u + 1], None, ALU.is_equal, ALU.add,
                                      accum_out=count[:, u:u + 1]).then_inc(e_twin_s, 1)
                    dve.wait_ge(e_twin_s, n + 1)
                    dve.tensor_scalar(again[:, u:u + 1], count[:, u:u + 1], -1.0, k.second[:, 0:1], ALU.add, ALU.mult).then_inc(e_again_s, 1)
                    dve.wait_ge(e_again_s, n + 1)
                    if later(n, 2):
                        dve.wait_ge(e_added, 16 * (n - 1))
                    dve.scalar_tensor_tensor(out=to[:, u:u + 1], in0=column_of(k.move, n), scalar=again[:, u:u + 1], in1=tok[:, u:u + 1],
                                             op0=ALU.mult, op1=ALU.add).then_inc(e_to_s, 1)
                if on[1]:
                    dve.wait_ge(e_y, j + 1)
                    dve.wait_ge(e_wcol_s, 2 * j + 2)
                    if later(j, 2):
                        dve.wait_ge(e_sum, j - 1)
                    dve.tensor_scalar(part[:, v, :], b_y[:, 0:D], wcol[:, v:v + 1], None, ALU.mult).then_inc(e_part_s, 1)
            pipelined(dve, step, NP_E, 3)
        inner.close()
        z.end()


def over_rows(vector, rows=P):
    return vector.rearrange("(a d) -> a d", a=1).to_broadcast([rows, vector.shape[0]])


def program(nc, ins, out, table):
    with ExitStack() as stack:
        z = Scope(nc, stack)
        bank = [stack.enter_context(nc.psum_tensor(f"bank{i}", [P, BANK], F32)) for i in range(8)]
        k = Shared()
        k.xres = z.sb("xres", [P, NT, D])
        k.raw = z.sb("raw", [P, NT, 6])
        k.mean2, k.apart, k.square = z.sb("mean2", [P, NT]), z.sb("apart", [P, NT]), z.sb("square", [P, NT])
        k.spread2, k.var, k.lnv = z.sb("spread2", [P, NT]), z.sb("var", [P, NT]), z.sb("lnv", [P, NT])
        k.rstd, k.nmr = z.sb("rstd", [P, NT]), z.sb("nmr", [P, NT])
        k.ident = z.sb("ident", [P, P])
        k.ln_eps = z.sb("ln_eps", [P, 1])
        k.loaded = stack.enter_context(nc.semaphore("loaded"))
        k.w1, k.b1 = z.sb("w1", [P, KC, F]), z.sb("b1", [P, FC])
        k.w2, k.b2 = z.sb("w2", [P, FC, D]), z.sb("b2", [P, D])
        k.w_r, k.b_r = z.sb("w_r", [P, D]), z.sb("b_r", [P, 1])
        k.same, k.earlier, k.slot = z.sb("same", [P, P]), z.sb("earlier", [P, P]), z.sb("slot", [P, 2 * KEEP])
        k.later_loads = [
            (k.w1[:, :, :], ins["L0_ffn_w1"].rearrange("(c p) n -> p c n", p=P)), (k.b1[:, :], ins["ffn_b1_columns"]),
            (k.w2[:, :, :], ins["L0_ffn_w2"].rearrange("(c p) n -> p c n", p=P)), (k.b2[:, :], over_rows(ins["L0_ffn_b2"])),
            (k.w_r[:, :], over_rows(ins["L0_ffn_w_r"])), (k.b_r[:, :], over_rows(ins["ffn_b_r"])),
            (k.same[:, :], ins["same_batch"]), (k.earlier[:, :], ins["earlier"]), (k.slot[:, :], ins["slot"])]
        k.wq1, k.wo1 = z.sb("wq1", [P, KC, D]), z.sb("wo1", [P, KC, D])
        k.wk1, k.wv1, k.wkv1d = z.sb("wk1", [P, D]), z.sb("wv1", [P, D]), z.sb("wkv1d", [P, 2 * D])
        k.bqk1 = z.sb("bqk1", [P, 2 * D])
        k.bv1, k.bv1d, k.bo1 = z.sb("bv1", [P, D]), z.sb("bv1d", [P, D]), z.sb("bo1", [P, D])
        k.norms, k.kind, k.head_mask1 = z.sb("norms", [P, 6]), z.sb("kind", [P, 2]), z.sb("head_mask1", [P, HG1])
        k.later_loads += [
            (k.wq1[:, :, :], ins["L1_xattn_Wq"].rearrange("(c p) n -> p c n", p=P)),
            (k.wo1[:, :, :], ins["L1_xattn_Wo"].rearrange("(c p) n -> p c n", p=P)),
            (k.wk1[:, :], ins["main_k_w"]), (k.wv1[:, :], ins["main_v_w"]), (k.wkv1d[:, :], ins["L1_xattn_Wkv_dca"]),
            (k.bqk1[:, 0:D], over_rows(ins["L1_xattn_bq"])), (k.bqk1[0:2 * MAIN, D:2 * D], over_rows(ins["main_k_b"], 2 * MAIN)),
            (k.bqk1[2 * MAIN:P, D:2 * D], over_rows(ins["L1_xattn_bkv_dca"][0:D], 2 * DCA)),
            (k.bv1[:, :], over_rows(ins["main_v_b"])), (k.bv1d[:, :], over_rows(ins["L1_xattn_bkv_dca"][D:2 * D])),
            (k.bo1[:, :], over_rows(ins["L1_xattn_bo"])), (k.norms[:, :], ins["head_norms"]), (k.kind[:, :], ins["key_kind"]),
            (k.head_mask1[:, :], ins["head_mask1"])]
        k.gate = z.sb("gate", [P, KC, E])
        k.countdown = z.sb("countdown", [P, NT])
        k.row_number, k.spare_row, k.second = z.sb("row_number", [P, 1]), z.sb("spare_row", [P, 1]), z.sb("second", [P, 1])
        k.token, k.move = z.sb("token", [P, NP_E]), z.sb("move", [P, NP_E])
        k.later_loads += [
            (k.gate[:, :, :], ins["gate_t"].rearrange("(c p) e -> p c e", p=P)), (k.countdown[:, :], ins["countdown"]),
            (k.row_number[:, :], ins["row_number"]), (k.spare_row[:, :], ins["spare_row"]), (k.second[:, :], ins["second"])]
        first_attention(nc, ins, k, bank)
        kept_feed_forward(nc, ins, k, bank)
        second_attention(nc, ins, k, bank)
        with nc.sbuf_tensor("found", [P, T // 2], F32) as found:
            k.found = found
            route(nc, ins, k, bank, out, table)
            fill_slots(nc, ins, k, bank)
        experts(nc, ins, k, bank, out, table)


def shape_constants():
    p = np.arange(P)
    d = p % HD0
    freq = (ROPE_BASE ** (-np.arange(2, dtype=np.float32) / 2)).astype(np.float32)
    freq4 = np.zeros((4, P), np.float32)
    freq4[2 * (p // 64) + d // 4, p] = freq[(d % 4) // 2]
    same = (p[:, None] // S == p // S).astype(np.float32)
    kept = np.arange(2 * KEEP)
    return {
        "ident": np.eye(P, dtype=np.float32),
        "freq4": freq4,
        "rope_sign": np.where(d % 2 == 0, -1.0, 1.0).astype(np.float32)[:, None],
        "head_mask0": (((p % 64) // HD0)[:, None] == np.arange(HG0)).astype(np.float32) / np.sqrt(np.float32(HD0)),
        "head_mask1": ((p // HD1)[:, None] == np.arange(HG1)).astype(np.float32) * np.float32(HD1) ** np.float32(-0.5),
        "key_kind": np.stack([p % S < MAIN, p % S >= MAIN], axis=1).astype(np.float32),
        "countdown": (T - P * np.arange(NT)[None, :] - p[:, None]).astype(np.float32),
        "row_number": p[:, None].astype(np.float32),
        "spare_row": (T + p)[:, None].astype(np.float32),
        "second": (p >= CAP)[:, None].astype(np.float32),
        "same_batch": same,
        "earlier": same * (p[None, :] < p[:, None]).astype(np.float32),
        "slot": np.where(p[:, None] // S == kept // KEEP, kept % KEEP, -1).astype(np.float32),
    }


def swap_pairs(w):
    return np.ascontiguousarray(w.reshape(w.shape[0], -1, 2)[:, :, ::-1].reshape(w.shape))


def lay_out(a):
    laid = {n: v for n, v in a.items() if n not in ("ctx_1024", "fside_BxSx2_0", "L0_ffn_b_r", "L0_ffn_b1")}
    laid["ctx_t"] = np.ascontiguousarray(a["ctx_1024"].reshape(T, C).T)
    laid["pos4"] = np.ascontiguousarray(a["fside_BxSx2_0"].reshape(NT, 2, S, 2).transpose(1, 3, 0, 2).reshape(4, NT * S))
    laid["wq_swapped"] = swap_pairs(a["L0_xattn_Wq"])
    laid["wk_swapped"] = swap_pairs(a["L0_xattn_Wkv"][:, 0:D])
    laid["ffn_b1_columns"] = np.ascontiguousarray(a["L0_ffn_b1"].reshape(FC, P).T)
    laid["ffn_b_r"] = a["L0_ffn_b_r"].reshape(1)
    by_kind = laid["ctx_t"].reshape(C, NT, 2, S)
    laid["ctx_keys_t"] = np.ascontiguousarray(np.concatenate(
        [by_kind[..., :MAIN].reshape(C, NT, 2 * MAIN), by_kind[..., MAIN:].reshape(C, NT, 2 * DCA)], axis=2).reshape(C, T))
    for part, left, right in (("w", "L1_xattn_Wk", "L1_xattn_Wv"), ("b", "L1_xattn_bk", "L1_xattn_bv")):
        both = np.concatenate([np.asarray(laid.pop(left)), np.asarray(laid.pop(right))], axis=-1)
        heads = both.reshape(both.shape[:-1] + (H1, 2, HD1))
        for n, name in enumerate(("main_k_", "main_v_")):
            laid[name + part] = np.ascontiguousarray(heads[..., n, :]).reshape(both.shape[:-1] + (D,))
    laid["gate_t"] = np.ascontiguousarray(laid.pop("L1_ffn_gate_w").T)
    laid["head_norms"] = np.ascontiguousarray(np.stack(
        [np.tile(a[f"L1_xattn_{n}"], P // HD1) for n in ("qn_w", "qn_b", "kn_w", "kn_b", "kn_dca_w", "kn_dca_b")], axis=1))
    laid.update(shape_constants())
    return laid


def kernel(**inputs):
    from concourse import bacc
    from concourse.bass_utils import run_bass_kernel_spmd

    nc = bacc.Bacc("TRN2", target_bir_lowering=False, num_devices=1)
    laid = lay_out({n: np.asarray(v) for n, v in inputs.items()})
    arrays = {f"in_{n}": np.ascontiguousarray(v) for n, v in laid.items()}
    ins = {n: nc.dram_tensor(f"in_{n}", v.shape, mybir.dt.from_np(v.dtype), kind="ExternalInput").ap()
           for n, v in laid.items()}
    out = nc.dram_tensor("out", [T + P, D], F32, kind="ExternalOutput").ap()
    table = nc.dram_tensor("table", [T + P, ROW], F32, kind="Internal").ap()
    program(nc, ins, out, table)
    r = run_bass_kernel_spmd(nc, [arrays], core_ids=[0])
    return r.results[0]["out"][0:T].reshape(B, S, D)
```
